# Optimizing a Trainium2 kernel written in Bass

```python
import numpy as np
import jax
import jax.numpy as jnp

def _softmax(x, axis=-1):
    return jax.nn.softmax(x, axis=axis)

def _gelu(x):
    return jax.nn.gelu(x, approximate=True)

def _silu(x):
    return jax.nn.silu(x)

def _sigmoid(x):
    return jax.nn.sigmoid(x)

def _layernorm(x, axis=-1, eps=1e-05):
    m = jnp.mean(x, axis=axis, keepdims=True)
    v = jnp.var(x, axis=axis, keepdims=True)
    return (x - m) / jnp.sqrt(v + eps)

def _scatter_add(tgt, idx, src, axis=0):
    return tgt.at[idx].add(src)

def _segment_sum(src, seg, n):
    return jax.ops.segment_sum(src, seg, n)
kernel_name = 'mk_decoder_preln_d1_seqx_r8_3aeb18'

def setup_inputs(seed: int=0):
    np.random.seed(seed)
    _w = jnp.asarray

    def _rec_inputs():
        import jax
        import jax.numpy as jnp
        _rk = jax.random.key(seed)
        x = 7.22e-05 + 1 * jax.random.normal(jax.random.fold_in(_rk, 1), (128, 64, 128), jnp.float32)
        _lenS = 64 - jax.random.randint(jax.random.fold_in(_rk, 7), (128,), 0, max(1, 64 // 4) + 1, jnp.int32)
        _lenS2 = 64 - jax.random.randint(jax.random.fold_in(_rk, 8), (128,), 0, max(1, 64 // 4) + 1, jnp.int32)
        _ctx_1024P = jax.random.normal(jax.random.fold_in(_rk, 11), (128, 16, 128), jnp.float32)
        _ctx_1024c = jax.random.dirichlet(jax.random.fold_in(_rk, 511), 0.3 * jnp.ones((16,), jnp.float32), (128, 64))
        _ctx_1024t = jnp.einsum('bsk,bkd->bsd', _ctx_1024c, _ctx_1024P)
        _ctx_1024t = _ctx_1024t * jax.lax.rsqrt(jnp.mean(jnp.square(_ctx_1024t)) + 1e-12) * 0.953939
        ctx_1024 = 4.13588e-05 + 0.999923 * (_ctx_1024t + 0.3 * jax.random.normal(jax.random.fold_in(_rk, 611), (128, 64, 128), jnp.float32))
        _validS = jnp.arange(64)[None, :] < _lenS[:, None]
        _validS2 = jnp.arange(64)[None, :] < _lenS2[:, None]
        _causal = jnp.tril(jnp.ones((64, 64), dtype=bool))
        mask_1x1xSxS2_ik0 = jnp.where(jnp.broadcast_to(_validS2[0:1, None, None, :], (1, 1, 64, 64)), 0, 1).astype(jnp.int32)
        return (x, ctx_1024, mask_1x1xSxS2_ik0)
    x, ctx_1024, mask_1x1xSxS2_ik0 = _rec_inputs()

    def _L0_attn_setup():
        import jax, jax.numpy as jnp
        import numpy as np
        MODEL_DIM = 128
        HEADS = 16
        HEAD_DIM = MODEL_DIM // HEADS
        B, T = (2, 256)
        TB_LEN = 500
        key = jax.random.key(seed)
        ks = jax.random.split(key, 12)
        s = 0.02
        d = MODEL_DIM
        return {'x': jax.random.normal(ks[0], (B, T, d), dtype=jnp.float32), 'Wq': jax.random.normal(ks[1], (d, d), dtype=jnp.float32) * s, 'bq': jnp.zeros((d,), jnp.float32), 'Wk': jax.random.normal(ks[2], (d, d), dtype=jnp.float32) * s, 'bk': jnp.zeros((d,), jnp.float32), 'Wv': jax.random.normal(ks[3], (d, d), dtype=jnp.float32) * s, 'bv': jnp.zeros((d,), jnp.float32), 'Wo': jax.random.normal(ks[4], (d, d), dtype=jnp.float32) * s, 'bo': jnp.zeros((d,), jnp.float32), 'et_gate': jax.random.normal(ks[5], (1, 1, 1), dtype=jnp.float32), 'is_gate': jax.random.normal(ks[6], (1, 1, 1), dtype=jnp.float32), 'time_bias': jnp.linspace(-1.0, 1.0, TB_LEN, dtype=jnp.float32).reshape(1, 1, TB_LEN)}
    _L0_attn_all = _L0_attn_setup()
    _L0_attn_in = {k: v for k, v in _L0_attn_all.items() if k in ('Wq', 'bq', 'Wk', 'bk', 'Wv', 'bv', 'Wo', 'bo', 'et_gate', 'is_gate', 'time_bias')}
    del _L0_attn_all

    def _L0_xattn_setup():
        import jax, jax.numpy as jnp
        import numpy as np
        import math
        D_MODEL = 128
        N_HEADS = 16
        D_HEAD = D_MODEL // N_HEADS
        B, S = (4, 256)
        key = jax.random.key(seed)
        ks = jax.random.split(key, 11)
        sc = 1.0 / math.sqrt(D_MODEL)
        inp = {'query': jax.random.normal(ks[0], (B, S, D_MODEL), jnp.float32), 'key': jax.random.normal(ks[1], (B, S, D_MODEL), jnp.float32), 'value': jax.random.normal(ks[2], (B, S, D_MODEL), jnp.float32), 'mask': jnp.tril(jnp.ones((S, S), jnp.int32))[None, None, :, :], 'wq': jax.random.normal(ks[3], (D_MODEL, D_MODEL), jnp.float32) * sc, 'bq': jax.random.normal(ks[4], (D_MODEL,), jnp.float32) * sc, 'wk': jax.random.normal(ks[5], (D_MODEL, D_MODEL), jnp.float32) * sc, 'bk': jax.random.normal(ks[6], (D_MODEL,), jnp.float32) * sc, 'wv': jax.random.normal(ks[7], (D_MODEL, D_MODEL), jnp.float32) * sc, 'bv': jax.random.normal(ks[8], (D_MODEL,), jnp.float32) * sc, 'wo': jax.random.normal(ks[9], (D_MODEL, D_MODEL), jnp.float32) * sc, 'bo': jax.random.normal(ks[10], (D_MODEL,), jnp.float32) * sc}
        return inp
    _L0_xattn_all = _L0_xattn_setup()
    _L0_xattn_in = {k: v for k, v in _L0_xattn_all.items() if k in ('wq', 'bq', 'wk', 'bk', 'wv', 'bv', 'wo', 'bo')}
    del _L0_xattn_all

    def _L0_ffn_setup():
        import jax, jax.numpy as jnp
        import numpy as np
        key = jax.random.key(seed)
        k0, k1, k2, k3 = jax.random.split(key, 4)
        B, S, D, F, E = (8, 256, 128, 256, 8)
        x = jax.random.normal(k0, (B, S, D), dtype=jnp.float32)
        Wg = jax.random.normal(k1, (D, E), dtype=jnp.float32) * 0.02
        W1 = jax.random.normal(k2, (E, D, F), dtype=jnp.float32) * 0.02
        W2 = jax.random.normal(k3, (E, F, D), dtype=jnp.float32) * 0.02
        return {'x': x, 'Wg': Wg, 'W1': W1, 'W2': W2}
    _L0_ffn_all = _L0_ffn_setup()
    _L0_ffn_in = {k: v for k, v in _L0_ffn_all.items() if k in ('Wg', 'W1', 'W2')}
    del _L0_ffn_all
    return {'x': x, 'ctx_1024': ctx_1024, 'mask_1x1xSxS2_ik0': mask_1x1xSxS2_ik0, 'L0_attn_Wq': _L0_attn_in['Wq'], 'L0_attn_bq': _L0_attn_in['bq'], 'L0_attn_Wk': _L0_attn_in['Wk'], 'L0_attn_bk': _L0_attn_in['bk'], 'L0_attn_Wv': _L0_attn_in['Wv'], 'L0_attn_bv': _L0_attn_in['bv'], 'L0_attn_Wo': _L0_attn_in['Wo'], 'L0_attn_bo': _L0_attn_in['bo'], 'L0_attn_et_gate': _L0_attn_in['et_gate'], 'L0_attn_is_gate': _L0_attn_in['is_gate'], 'L0_attn_time_bias': _L0_attn_in['time_bias'], 'L0_xattn_wq': _L0_xattn_in['wq'], 'L0_xattn_bq': _L0_xattn_in['bq'], 'L0_xattn_wk': _L0_xattn_in['wk'], 'L0_xattn_bk': _L0_xattn_in['bk'], 'L0_xattn_wv': _L0_xattn_in['wv'], 'L0_xattn_bv': _L0_xattn_in['bv'], 'L0_xattn_wo': _L0_xattn_in['wo'], 'L0_xattn_bo': _L0_xattn_in['bo'], 'L0_ffn_Wg': _L0_ffn_in['Wg'], 'L0_ffn_W1': _L0_ffn_in['W1'], 'L0_ffn_W2': _L0_ffn_in['W2']}

def reference(x, ctx_1024, mask_1x1xSxS2_ik0, L0_attn_Wq, L0_attn_bq, L0_attn_Wk, L0_attn_bk, L0_attn_Wv, L0_attn_bv, L0_attn_Wo, L0_attn_bo, L0_attn_et_gate, L0_attn_is_gate, L0_attn_time_bias, L0_xattn_wq, L0_xattn_bq, L0_xattn_wk, L0_xattn_bk, L0_xattn_wv, L0_xattn_bv, L0_xattn_wo, L0_xattn_bo, L0_ffn_Wg, L0_ffn_W1, L0_ffn_W2):
    import jax
    import jax.numpy as jnp

    def _L0_attn_ref(x, Wq, bq, Wk, bk, Wv, bv, Wo, bo, et_gate, is_gate, time_bias):
        import jax, jax.numpy as jnp
        import numpy as np
        MODEL_DIM = 128
        HEADS = 16
        HEAD_DIM = MODEL_DIM // HEADS
        B, T = (2, 256)
        TB_LEN = 500
        Bb, Tt, D = x.shape
        H, hd = (HEADS, HEAD_DIM)
        Q = (x @ Wq.T + bq).reshape(Bb, Tt, H, hd).transpose(0, 2, 1, 3)
        K = (x @ Wk.T + bk).reshape(Bb, Tt, H, hd).transpose(0, 2, 1, 3)
        V = (x @ Wv.T + bv).reshape(Bb, Tt, H, hd).transpose(0, 2, 1, 3)
        scores = jnp.einsum('bhqd,bhkd->bhqk', Q, K) / jnp.sqrt(jnp.float32(hd))
        pos = jnp.arange(Tt)[None, :] - jnp.arange(Tt)[:, None]
        idx = jnp.clip(pos + TB_LEN // 2, 0, TB_LEN - 1)
        tp = time_bias[:, :, idx]
        tp = jnp.squeeze(tp, axis=1)[None, None]
        scores = scores + jax.nn.sigmoid(et_gate) * tp + is_gate
        attn = jax.nn.softmax(scores, axis=-1)
        context = jnp.matmul(attn, V)
        context = context.transpose(0, 2, 1, 3, 4).reshape(Bb, Tt, D)
        return context @ Wo.T + bo

    def _L0_xattn_ref(query, key, value, mask, wq, bq, wk, bk, wv, bv, wo, bo):
        import jax, jax.numpy as jnp
        import numpy as np
        import math
        D_MODEL = 128
        N_HEADS = 16
        D_HEAD = D_MODEL // N_HEADS
        B, S = (4, 256)
        b, s, _ = query.shape
        q = query @ wq.T + bq
        k = key @ wk.T + bk
        v = value @ wv.T + bv
        q = q.reshape(b, s, N_HEADS, D_HEAD).transpose(0, 2, 1, 3)
        k = k.reshape(b, s, N_HEADS, D_HEAD).transpose(0, 2, 1, 3)
        v = v.reshape(b, s, N_HEADS, D_HEAD).transpose(0, 2, 1, 3)
        scores = jnp.einsum('bhqd,bhkd->bhqk', q, k) / math.sqrt(D_HEAD)
        scores = jnp.where(mask == 0, jnp.float32(-1000000000.0), scores)
        attn = jax.nn.softmax(scores, axis=-1)
        out = jnp.einsum('bhqk,bhkd->bhqd', attn, v)
        out = out.transpose(0, 2, 1, 3).reshape(b, s, D_MODEL)
        return out @ wo.T + bo

    def _L0_ffn_ref(x, Wg, W1, W2):
        import jax, jax.numpy as jnp
        import numpy as np
        B, S, D = x.shape
        E = Wg.shape[1]
        T = B * S
        cap = max(1, T // E)
        xt = x.reshape(T, D)
        logits = xt @ Wg
        probs = jax.nn.softmax(logits, axis=-1)
        pT = probs.T
        _, top_idx = jax.lax.top_k(pT, cap)
        sel = jnp.zeros((E, T), dtype=bool).at[jnp.arange(E)[:, None], top_idx].set(True)
        masked = jnp.where(sel, pT, -jnp.inf)
        assigned = sel.any(axis=0)
        tok2exp = jnp.where(assigned, jnp.argmax(masked, axis=0), jnp.argmax(pT, axis=0))
        weights = jnp.take_along_axis(probs, tok2exp[:, None], axis=1)[:, 0]
        out = jnp.zeros_like(xt)
        for e in range(E):
            gate = jnp.where(tok2exp == e, weights, 0.0)
            h = jax.nn.gelu(xt @ W1[e], approximate=False) @ W2[e]
            out = out + gate[:, None] * h
        return out.reshape(B, S, D)
    x = x + _L0_attn_ref(_layernorm(x, axis=-1), L0_attn_Wq, L0_attn_bq, L0_attn_Wk, L0_attn_bk, L0_attn_Wv, L0_attn_bv, L0_attn_Wo, L0_attn_bo, L0_attn_et_gate, L0_attn_is_gate, L0_attn_time_bias)
    x = x + _L0_xattn_ref(_layernorm(x, axis=-1), ctx_1024, ctx_1024, mask_1x1xSxS2_ik0, L0_xattn_wq, L0_xattn_bq, L0_xattn_wk, L0_xattn_bk, L0_xattn_wv, L0_xattn_bv, L0_xattn_wo, L0_xattn_bo)
    x = x + _L0_ffn_ref(_layernorm(x, axis=-1), L0_ffn_Wg, L0_ffn_W1, L0_ffn_W2)
    return x

_drawn_inputs = setup_inputs


def setup_inputs(seed=0):
    import zlib

    import numpy as np

    out = dict(_drawn_inputs(seed))
    spreads = {'L0_attn_bq': (0.0, 0.8),
     'L0_attn_bk': (0.0, 0.8),
     'L0_attn_bv': (0.0, 0.42),
     'L0_attn_bo': (0.0, 0.1)}
    factors = {'L0_attn_Wq': 8.0,
     'L0_attn_Wk': 8.0,
     'L0_attn_Wv': 8.0,
     'L0_attn_Wo': 2.783,
     'L0_attn_time_bias': 8.0,
     'L0_xattn_bk': 8.0,
     'L0_ffn_Wg': 8.0,
     'L0_ffn_W1': 8.0,
     'L0_ffn_W2': 8.0}
    for name, (base, spread) in spreads.items():
        noise = np.random.default_rng([zlib.crc32(name.encode()), seed]).standard_normal(out[name].shape)
        drawn = base * np.exp(spread * noise) if base else spread * noise
        out[name] = jnp.asarray(drawn.astype(out[name].dtype))
    for name, factor in factors.items():
        out[name] = (out[name] * factor).astype(out[name].dtype)
    return out
```

```python
from contextlib import ExitStack

import concourse.bass as bass
from concourse import mybir

F32 = mybir.dt.float32
BF16 = mybir.dt.bfloat16
I32 = mybir.dt.int32
ALU = mybir.AluOpType
ACT = mybir.ActivationFunctionType
AX = mybir.AxisListType

P = 128
B, T, D = 128, 64, 128
H, HD = 16, 8
C = P // 32
G = H // C
NPAIR = C // 2
UB = 8
UNITS = B // UB
UT = UB * T // P
SW = G * T
OW = HD + 1
OB = H * OW
E, FF = 8, 256
TILES = B * T // P
CAP = B * T // E
EPS = 1e-5
MASKED = -1e30


def known(v):
    return isinstance(v, int)


def wait(eng, sem, value):
    if not known(value) or value > 0:
        eng.wait_ge(sem, value)


def wait_apart(eng, sem, value):
    wait(eng, sem, value)
    if not known(value):
        eng.nop(nofuse=True)


def live(n, count):
    return not known(n) or 0 <= n < count


def units(eng, unit):
    unit(-1, 1)
    unit(0, 0)
    unit(1, 1)
    with eng.Fori(1, UNITS // 2 - 1) as k:
        unit(2 * k, 0)
        unit(2 * k + 1, 1)
    unit(UNITS - 2, 0)
    unit(UNITS - 1, 1)
    unit(UNITS, 0)


NEWTON = 3


def guess_rstd(nc, dve, var, veps, guess, moments_ready, guessed, i):
    dve.wait_ge(moments_ready, UT * (i + 1))
    nc.vector.tensor_scalar(veps, var, EPS, None, ALU.add).then_inc(guessed, 1)
    dve.wait_ge(guessed, 3 * i + 1)
    nc.vector.tensor_scalar(guess.bitcast(I32), veps.bitcast(I32), 1, None, ALU.arith_shift_right).then_inc(guessed, 1)
    dve.wait_ge(guessed, 3 * i + 2)
    nc.vector.tensor_scalar(guess.bitcast(I32), guess.bitcast(I32), -1.0, float(0x5F3759DF), ALU.mult, ALU.add).then_inc(guessed, 1)


def refine_rstd(nc, pool, veps, y, t, guessed, refined, i):
    wait_apart(pool, guessed, 3 * i + 3)
    for k in range(NEWTON):
        done = 4 * NEWTON * i + 4 * k
        if k:
            wait_apart(pool, refined, done)
        nc.gpsimd.tensor_tensor(t, y, y, ALU.mult).then_inc(refined, 1)
        wait_apart(pool, refined, done + 1)
        nc.gpsimd.tensor_tensor(t, t, veps, ALU.mult).then_inc(refined, 1)
        wait_apart(pool, refined, done + 2)
        nc.gpsimd.tensor_scalar(t, t, -0.5, 1.5, ALU.mult, ALU.add).then_inc(refined, 1)
        wait_apart(pool, refined, done + 3)
        nc.gpsimd.tensor_tensor(y, y, t, ALU.mult).then_inc(refined, 1)


class Memory:

    def __init__(self, nc):
        self.nc = nc
        self.ctx = ExitStack()

    def sb(self, name, shape, dt=F32):
        return self.ctx.enter_context(self.nc.sbuf_tensor(name, shape, dt))

    def ps(self, name, shape, dt=F32):
        return self.ctx.enter_context(self.nc.psum_tensor(name, shape, dt))

    def sem(self, name):
        return self.ctx.enter_context(self.nc.semaphore(name))


def setup(nc, a, m):
    with ExitStack() as stack:
        s = Memory(nc)
        stack.enter_context(s.ctx)
        loaded, zeroed, placed = s.sem("loaded"), s.sem("zeroed"), s.sem("placed")
        gate, table, tmask, parts = (s.sem(n) for n in ("gate_ready", "table_ready", "mask_ready", "parts_ready"))
        block = stack.enter_context(nc.Block())
        loads = [
            (m.ident[:, :], a["ident"]),
            (m.qscale[:, :], a["class_scale"]),
            (m.dupf[:, :], a["dup"]),
            (m.before[:, :], a["before"]),
            (m.wg[:, :], a["wg"]),
            (m.tb[:, :], a["time_tile"]),
            (m.gates[:, 0:1], a["et_gate"].partition_broadcast(P)),
            (m.gates[:, 1:2], a["is_gate"].partition_broadcast(P)),
            (m.maski[:, :], a["mask_tile"]),
            (m.bo_row[:, 0, :], a["self_bo"].partition_broadcast(P)),
            (m.bo_row[:, 1, :], a["cross_bo"].partition_broadcast(P)),
            (m.w2o[:, :], a["cross_wo"]),
        ]
        for n, who in enumerate(("self", "cross")):
            loads += [(m.wqkv[:, n, w, :], a[f"{who}_w{x}"]) for w, x in enumerate("qkv")]
            loads += [(m.bqk[:, n, w:w + 1], a[f"{who}_b{x}"]) for w, x in enumerate("qk")]
            loads += [(m.bv[64 * gh:64 * gh + 64, n, :], a[f"{who}_bv"][gh].partition_broadcast(64)) for gh in range(2)]

        @block.sync
        def _(sp):
            for out, in_ in loads:
                sp.dma_start(out, in_).then_inc(loaded, 16)
            sp.wait_ge(zeroed, 1)
            for jq in range(8):
                sp.dma_start(m.wexp[16 * jq:16 * jq + 16, :, jq * D:(jq + 1) * D], a["self_wo"]).then_inc(placed, 16)
            sp.wait_ge(loaded, 16 * len(loads))
            sp.wait_ge(placed, 16 * 8)

        @block.gpsimd
        def _(pool):
            nc.gpsimd.memset(m.wexp[:, :, :], 0.0).then_inc(zeroed, 1)
            nc.gpsimd.memset(m.kexp[:, :, :, :, :], 0.0).then_inc(zeroed, 1)
            nc.gpsimd.memset(m.vb[:, :, :, :, :, :], 0.0).then_inc(zeroed, 1)
            pool.wait_ge(zeroed, 3)
            for gh in range(2):
                nc.gpsimd.memset(m.vb[64 * gh:64 * gh + 64, :, :, :, gh, HD:OW], 1.0).then_inc(zeroed, 1)

        @block.scalar
        def _(act):
            act.wait_ge(loaded, 16 * len(loads))
            nc.scalar.activation(m.gates[:, 2:3], m.gates[:, 0:1], ACT.Sigmoid).then_inc(gate, 1)

        @block.vector
        def _(dve):
            dve.wait_ge(loaded, 16 * len(loads))
            nc.vector.tensor_copy(m.dup[:, :], m.dupf[:, :])
            nc.vector.memset(m.ones[:, :], 1.0)
            nc.vector.memset(m.onesb[:, :], 1.0)
            nc.vector.tensor_copy(m.beforeb[:, :], m.before[:, :])
            nc.vector.tensor_copy(m.maskf[:, :], m.maski[:, :]).then_inc(tmask, 1)
            dve.wait_ge(tmask, 1)
            nc.vector.tensor_scalar(m.maskb[:, :], m.maskf[:, :], 0.0, MASKED, ALU.is_equal, ALU.mult).then_inc(tmask, 1)
            dve.wait_ge(gate, 1)
            nc.vector.tensor_scalar(m.tb[:, :], m.tb[:, :], m.gates[:, 2:3], m.gates[:, 1:2], ALU.mult, ALU.add).then_inc(table, 1)
            dve.wait_ge(table, 1)
            nc.vector.tensor_copy(m.tb_hi[:, :], m.tb[:, :]).then_inc(parts, 1)
            dve.wait_ge(parts, 1)
            nc.vector.tensor_tensor(m.tb_rest[:, :], m.tb[:, :], m.tb_hi[:, :], ALU.subtract).then_inc(parts, 1)
            dve.wait_ge(parts, 2)
            nc.vector.tensor_copy(m.tb_mid[:, :], m.tb_rest[:, :]).then_inc(parts, 1)
            dve.wait_ge(parts, 3)
            nc.vector.tensor_tensor(m.tb_lo[:, :], m.tb_rest[:, :], m.tb_mid[:, :], ALU.subtract).then_inc(parts, 1)
            nc.vector.tensor_copy(m.tb_hm[0:64, :], m.tb_hi[0:64, :]).then_inc(parts, 1)
            nc.vector.tensor_copy(m.tb_hm[64:128, :], m.tb_mid[64:128, :]).then_inc(parts, 1)
            dve.wait_ge(parts, 6)


def attention(nc, a, m, cross):
    n_att = 1 if cross else 0
    pre = "cross_" if cross else "self_"
    with ExitStack() as stack:
        s = Memory(nc)
        stack.enter_context(s.ctx)
        sem = lambda name: s.sem(pre + name)
        scores_ready, max_ready, shifted = sem("scores_ready"), sem("max_ready"), sem("shifted")
        probs_ready, turned, turned_copied = sem("probs_ready"), sem("turned"), sem("turned_copied")
        out_ready, recip_ready, out_read = sem("out_ready"), sem("recip_ready"), sem("out_read")
        x_loaded = [sem(f"x_loaded{u}") for u in range(2)]
        stats_ready, moments_ready, guessed, xn_ready = (sem(n) for n in ("stats_ready", "moments_ready", "guessed", "xn_ready"))
        refined = sem("refined")
        xt_ready, xt_copied = sem("xt_ready"), sem("xt_copied")
        q_done, q_ready, k_done, k_ready, v_done, v_ready = (sem(n) for n in ("q_done", "q_ready", "k_done", "k_ready", "v_done", "v_ready"))
        if cross:
            c_loaded = [sem(f"c_loaded{u}") for u in range(2)]
            y_copied, y_ready, x_biased, x1_ready, x1_biased = (sem(n) for n in ("y_copied", "y_ready", "x_biased", "x1_ready", "x1_biased"))
            ct_ready, ct_copied, c2_turned, c2_copied, o_ready, o_added = (sem(n) for n in ("ct_ready", "ct_copied", "c2_turned", "c2_copied", "o_ready", "o_added"))

        sc = [s.ps(f"{pre}sc{i}", [P, NPAIR, G, T]) for i in range(2)]
        pt = [s.ps(f"{pre}pt{i}", [P, 4, P]) for i in range(2)]
        po = [s.ps(f"{pre}po{i}", [P, 512]) for i in range(2)]
        job = [s.ps(f"{pre}job{i}", [P, 512]) for i in range(2)]
        xin = s.sb(pre + "xin", [P, 2, UT, D])
        xn = s.sb(pre + "xn", [P, UT, D])
        xnt = s.sb(pre + "xnt", [P, UT * P])
        stats = s.sb(pre + "stats", [P, UT, 6])
        moments = s.sb(pre + "moments", [P, UT, 2])
        rstd, veps, newton = (s.sb(pre + n, [P, UT]) for n in ("rstd", "veps", "newton"))
        mx = s.sb(pre + "mx", [P, 2, NPAIR * G])
        sh = s.sb(pre + "sh", [P, 4, NPAIR * G * T])
        pts = s.sb(pre + "pts", [P, 2, 4, P])
        rec = s.sb(pre + "rec", [P, 2, H // 2])
        if cross:
            cin = s.sb(pre + "cin", [P, 2, UT, D])
            ct = s.sb(pre + "ct", [P, UT * P])
            yctx = s.sb(pre + "yctx", [P, HD, B])
            c2 = s.sb(pre + "c2", [P, 2, UB, H // 2, HD])
            c2t = s.sb(pre + "c2t", [P, UB // 2, 2, T])
        kvt = ct if cross else xnt
        wq, wk, wv = (m.wqkv[:, n_att, w, :] for w in range(3))
        block = stack.enter_context(nc.Block())

        def po_view(pair):
            return po[pair % 2][:, 0:2 * OB].rearrange("p (b h j w) -> p b h j w", b=2, h=H // 2, j=2)

        def bank(j):
            return job[j % 2]

        @block.sync
        def _(sp):
            def unit(su, u):
                f, fu = su + 1, 1 - u
                if not live(f, UNITS):
                    return
                if cross:
                    wait(sp, x1_ready, f - 1)
                    sp.dma_start(xin[:, fu, :, :], a["x_rows"][bass.ds(f, 1)].rearrange("o b n -> (o b) n")
                                 .rearrange("b (q n) -> b q n", q=UT)).then_inc(x_loaded[fu], 16)
                    wait(sp, ct_ready, f - 1)
                    sp.dma_start(cin[:, fu, :, :], a["ctx_tiles"][bass.ds(f, 1)].rearrange("o t p n -> (o p) t n"))\
                        .then_inc(c_loaded[fu], 16)
                else:
                    wait(sp, xn_ready, UT * (f - 1))
                    sp.dma_start(xin[:, fu, :, :], a["x_tiles"][bass.ds(f, 1)].rearrange("o t p n -> (o p) t n"))\
                        .then_inc(x_loaded[fu], 16)
            units(sp, unit)

        @block.gpsimd
        def _(pool):
            def unit(su, u):
                f, fu = su + 1, 1 - u
                if not live(f, UNITS):
                    return
                if not cross:
                    refine_rstd(nc, pool, veps[:, :], rstd[:, :], newton[:, :], guessed, refined, f)
                    return
                if fu == 0:
                    wait(pool, y_ready, f)
                    nc.gpsimd.tensor_copy(yctx[:, :, :], m.ctx[:, bass.ds(pair_of(f), 1), :, :].rearrange("p o d b -> p (o d) b"))\
                        .then_inc(y_copied, 1)
                pool.wait_ge(x_loaded[fu], 16 * (pair_of(f) + 1))
                nc.gpsimd.tensor_tensor(xin[:, fu, :, :], xin[:, fu, :, :], bo_tiles(0), ALU.add).then_inc(x_biased, 1)
                refine_rstd(nc, pool, veps[:, :], rstd[:, :], newton[:, :], guessed, refined, f)
                pool.wait_ge(xn_ready, UT * (f + 1))
                row = m.x[:, bass.ds(f, 1), :, :].rearrange("p o q n -> p (o q) n")
                nc.gpsimd.tensor_tensor(row, row, bo_tiles(1), ALU.add).then_inc(x1_biased, 1)

            def bo_tiles(n):
                return m.bo_row[:, n, :].unsqueeze(1).broadcast_to([P, UT, D])

            last = [0]

            def pair_of(f):
                if known(f):
                    return f // 2
                return pairs[0]

            pairs = [None]

            unit(-1, 1)
            unit(0, 0)
            unit(1, 1)
            with pool.Fori(1, UNITS // 2 - 1) as k:
                pairs[0] = k
                unit(2 * k, 0)
                pairs[0] = k + 1
                unit(2 * k + 1, 1)
            unit(UNITS - 2, 0)
            unit(UNITS - 1, 1)

        @block.tensor
        def _(pe):
            def scores(n, c, su, u):
                if not live(n, B):
                    return
                wait(pe, shifted, n - 1)
                if c == 0:
                    wait(pe, q_ready, su + 1)
                    wait(pe, k_ready, G * (su + 1))
                for jj in range(NPAIR):
                    out = sc[c % 2][:, jj, :, :]
                    nc.tensor.matmul(out, m.qexp[:, u, c, 2 * jj:2 * jj + 2, :], m.kexp[:, u, c, :, :], start=True, stop=False)
                    if cross:
                        last = nc.tensor.matmul(out, m.dup[0:64, :], m.maskb[0:64, :].unsqueeze(1).broadcast_to([64, G, T]),
                                                start=False, stop=True)
                    else:
                        nc.tensor.matmul(out, m.dup[:, :], m.tb_hm[:, :].unsqueeze(1).broadcast_to([P, G, T]), start=False, stop=False)
                        last = nc.tensor.matmul(out, m.dup[0:64, :], m.tb_lo[0:64, :].unsqueeze(1).broadcast_to([64, G, T]),
                                                start=False, stop=True)
                last.then_inc(scores_ready, 1)

            def turn(n, c):
                if not live(n, B):
                    return
                wait(pe, probs_ready, n + 1)
                wait(pe, turned_copied, n - 1)
                for i in range(4):
                    last = nc.tensor.transpose(pt[c % 2][:, i, :], sh[:, c % 4, P * i:P * i + P], m.ident[:, :])
                last.then_inc(turned, 1)

            def values(n, c, u, su):
                if not live(n, B):
                    return
                wait(pe, turned_copied, n + 1)
                if c == 0:
                    wait(pe, v_ready, 2 * (su + 1))
                if c % 2 == 0:
                    wait(pe, out_read, n - 2)
                o = po_view(c // 2)
                for jj in range(NPAIR):
                    for gp in range(G // 2):
                        out = o[:, c % 2, 4 * gp + jj:4 * gp + jj + 3:2, :, :].rearrange("p g j w -> p j g w")
                        last = nc.tensor.matmul(out, pts[:, c % 2, 2 * jj + gp, :], m.vb[:, u, 4 * c + 2 * gp + jj, :, :, :],
                                                start=True, stop=True)
                last.then_inc(out_ready, 1)

            def turn_tiles(out, tiles, sem_):
                for t in range(UT):
                    last = nc.tensor.transpose(out[:, P * t:P * t + P], tiles[:, t, :], m.ident[:, :])
                last.then_inc(sem_, 1)

            def turn_x(f, fu, j):
                pe.wait_ge(xn_ready, UT * (f + 1))
                turn_tiles(bank(j), xn, xt_ready)

            def project_q(f, fu, j):
                pe.wait_ge(xt_copied, f + 1)
                nc.tensor.matmul(bank(j)[:, :], wq, xnt[:, :], start=True, stop=True).then_inc(q_done, 1)

            def project_k(f, fu, j):
                pe.wait_ge(ct_copied if cross else xt_copied, f + 1)
                if cross:
                    pe.wait_ge(xt_copied, f + 1)
                nc.tensor.matmul(bank(j)[:, :], wk, kvt[:, :], start=True, stop=True).then_inc(k_done, 1)

            def project_v(f, fu, j):
                pe.wait_ge(q_ready, f + 1)
                for gh in range(2):
                    w = wv.rearrange("p (gp g c) -> p gp g c", g=2, c=C * HD)[:, :, gh, :]
                    for b in range(UB):
                        last = nc.tensor.matmul(bank(j)[64 * gh:64 * gh + 64, T * b:T * b + T].rearrange("p (g c) -> p g c", g=G // 2),
                                                kvt[:, T * b:T * b + T], w, start=True, stop=True)
                last.then_inc(v_done, 1)

            def self_front(f, fu, c):
                if not live(f, UNITS):
                    return
                if c == 1:
                    wait(pe, k_ready, G * f)
                    turn_x(f, fu, 0)
                if c == 2:
                    wait(pe, v_ready, 2 * f)
                    project_q(f, fu, 1)
                if c == 3:
                    project_k(f, fu, 2)
                if c == 4:
                    project_v(f, fu, 3)

            def cross_front(f, fu, c):
                if live(f, UNITS):
                    if c == 0:
                        wait(pe, k_ready, G * f)
                        wait(pe, c2_copied, 4 * (f - 2))
                        pe.wait_ge(y_copied, f // 2 + 1 if known(f) else pair[0] + 1)
                        for d in range(HD):
                            last = nc.tensor.matmul(bank(0)[:, :], yctx[:, d, :], m.wexp[:, d, 512 * fu:512 * fu + 512],
                                                    start=(d == 0), stop=(d == HD - 1))
                        last.then_inc(y_ready, 1)
                    if c == 1:
                        wait(pe, v_ready, 2 * f)
                        wait(pe, o_added, f - 2)
                        pe.wait_ge(c_loaded[fu], 16 * ((f // 2 if known(f) else pair[0]) + 1))
                        turn_tiles(bank(1), cin[:, fu, :, :], ct_ready)
                    if c == 2:
                        turn_x(f, fu, 2)
                    if c == 3:
                        project_q(f, fu, 3)
                    if c == 4:
                        project_k(f, fu, 4)
                    if c == 5:
                        project_v(f, fu, 5)
                if live(f - 2, UNITS):
                    if c == 6:
                        wait(pe, k_ready, min(G * (f + 1), G * UNITS) if known(f) else G * (f + 1))
                        wait(pe, out_read, 8 * (f - 1))
                        wait(pe, c2_copied, 4 * (f - 2))
                        for t in range(UB // 2):
                            last = nc.tensor.transpose(bank(6)[:, P * t:P * t + P],
                                                       c2[:, fu, 2 * t:2 * t + 2, :, :].rearrange("p b h d -> p (b h d)"), m.ident[:, :])
                        last.then_inc(c2_turned, 1)
                    if c == 7:
                        wait(pe, v_ready, min(2 * (f + 1), 2 * UNITS) if known(f) else 2 * (f + 1))
                        wait(pe, o_added, f - 2)
                        wait(pe, c2_copied, 4 * (f - 1))
                        tok = c2t[:, :, :, :].rearrange("p b c (t q) -> p q (b c t)", q=UT)
                        for q in range(UT):
                            last = nc.tensor.matmul(bank(7)[:, D * q:D * q + D], tok[:, q, :], m.w2o[:, :],
                                                    start=True, stop=True)
                        last.then_inc(o_ready, 1)

            pair = [None]

            def unit(su, u):
                f, fu = su + 1, 1 - u
                for c in range(UB):
                    n = UB * su + c
                    scores(n, c, su, u)
                    turn(n - 2, (c - 2) % 8)
                    c3 = (c - 3) % 8
                    values(n - 3, c3, u if c >= 3 else fu, su if c >= 3 else su - 1)
                    (cross_front if cross else self_front)(f, fu, c)

            unit(-1, 1)
            unit(0, 0)
            unit(1, 1)
            with pe.Fori(1, UNITS // 2 - 1) as k:
                pair[0] = k
                unit(2 * k, 0)
                pair[0] = k + 1
                unit(2 * k + 1, 1)
            unit(UNITS - 2, 0)
            unit(UNITS - 1, 1)
            unit(UNITS, 0)

        @block.scalar
        def _(act):
            def unit(su, u):
                f, fu = su + 1, 1 - u
                for c in range(UB):
                    n = UB * su + c
                    if live(f, UNITS):
                        if cross and c == 2:
                            act.wait_ge(ct_ready, f + 1)
                            nc.scalar.activation(ct[:, :], bank(1)[:, :], ACT.Copy).then_inc(ct_copied, 1)
                        if c == (3 if cross else 2):
                            act.wait_ge(xt_ready, f + 1)
                            if cross:
                                nc.scalar.activation(xnt[:, :].rearrange("p (b q) -> p q b", q=UT),
                                                     bank(2)[:, :].rearrange("p (q b) -> p q b", q=UT), ACT.Copy).then_inc(xt_copied, 1)
                            else:
                                nc.scalar.activation(xnt[:, :], bank(0)[:, :], ACT.Copy).then_inc(xt_copied, 1)
                        if c == (5 if cross else 4):
                            act.wait_ge(k_done, f + 1)
                            for g in range(G):
                                r = slice(32 * g, 32 * g + 32)
                                nc.scalar.activation(m.kexp[r, fu, :, g, :],
                                                     bank(4 if cross else 2)[r, :].rearrange("p (b k) -> p b k", b=UB),
                                                     ACT.Identity, bias=m.bqk[r, n_att, 1:2]).then_inc(k_ready, 1)
                    if cross and c == 7 and live(f - 2, UNITS):
                        wait(act, c2_turned, f - 1)
                        wait(act, o_ready, f - 2)
                        for j in range(2):
                            for bp in range(2):
                                nc.scalar.activation(c2t[64 * j:64 * j + 64, :, bp, :],
                                                     bank(6)[64 * bp:64 * bp + 64, :].rearrange(
                                                         "p (b j q) -> p b j q", j=2, q=T)[:, :, j, :],
                                                     ACT.Copy).then_inc(c2_copied, 1)
                    if live(n - 2, B):
                        wait(act, turned, n - 1)
                        wait(act, out_ready, n - 3)
                        nc.scalar.activation(pts[:, c % 2, :, :], pt[c % 2][:, :, :], ACT.Copy).then_inc(turned_copied, 1)
                    if live(n, B):
                        wait(act, shifted, n + 1)
                        nc.scalar.activation(sh[:, c % 4, :], sh[:, c % 4, :], ACT.Exp).then_inc(probs_ready, 1)
            units(act, unit)

        @block.vector
        def _(dve):
            def x_tiles(f, fu):
                if cross:
                    return [m.x[:, bass.ds(f, 1), t, :].rearrange("p o n -> p (o n)") for t in range(UT)]
                return [xin[:, fu, t, :] for t in range(UT)]

            def moments_x(f, fu):
                src = x_tiles(f, fu)
                for t in range(UT):
                    nc.vector.bn_stats(stats[:, t, :], src[t]).then_inc(stats_ready, 1)
                for t in range(UT):
                    wait_apart(dve, stats_ready, UT * f + t + 1)
                    nc.vector.bn_aggr(moments[:, t, :], stats[:, t, :]).then_inc(moments_ready, 1)
                guess_rstd(nc, dve, moments[:, :, 1], veps[:, :], rstd[:, :], moments_ready, guessed, f)

            def norm_x(f, fu):
                dve.wait_ge(refined, 4 * NEWTON * (f + 1))
                wait(dve, xt_ready, f)
                src = x_tiles(f, fu)
                for t in range(UT):
                    nc.vector.tensor_scalar(xn[:, t, :], src[t], moments[:, t, 0:1], rstd[:, t:t + 1], ALU.subtract, ALU.mult)\
                        .then_inc(xn_ready, 1)

            def spread_q(f, fu, j):
                dve.wait_ge(q_done, f + 1)
                for c in range(C):
                    nc.vector.tensor_scalar(m.qexp[:, fu, :, c, :], bank(j)[:, :].rearrange("p (b q) -> p b q", b=UB),
                                            m.bqk[:, n_att, 0:1], m.qscale[:, c:c + 1], ALU.add, ALU.mult)\
                        .then_inc(*((q_ready, 1) if c == C - 1 else (q_part, 1)))

            q_part = sem("q_part")

            def spread_v(f, fu, j):
                dve.wait_ge(v_done, f + 1)
                for gh in range(2):
                    r = slice(64 * gh, 64 * gh + 64)
                    view = lambda t: t.rearrange("p (x c d) -> p x c d", c=C, d=HD)
                    out = m.vb[r, fu, :, :, gh, 0:HD].rearrange("p (x j) c d -> p x (j c) d", j=NPAIR)
                    nc.vector.tensor_tensor(out, view(bank(j)[r, :]), view(m.bv[r, n_att, :]), ALU.add).then_inc(v_ready, 1)

            def front(f, fu, c):
                if not live(f, UNITS):
                    return
                if cross:
                    if c == 1:
                        dve.wait_ge(y_ready, f + 1)
                        dve.wait_ge(x_biased, f + 1)
                        nc.vector.tensor_tensor(m.x[:, bass.ds(f, 1), :, :].rearrange("p o q n -> p (o q n)"), bank(0)[:, :],
                                                xin[:, fu, :, :].rearrange("p q n -> p (q n)"), ALU.add).then_inc(x1_ready, 1)
                        wait_apart(dve, x1_ready, f + 1)
                        moments_x(f, fu)
                    if c == 2:
                        norm_x(f, fu)
                    if c == 4:
                        spread_q(f, fu, 3)
                    if c == 6:
                        spread_v(f, fu, 5)
                else:
                    if c == 0:
                        dve.wait_ge(x_loaded[fu], 16 * (f // 2 + 1 if known(f) else pair[0] + 1))
                        moments_x(f, fu)
                    if c == 1:
                        norm_x(f, fu)
                    if c == 3:
                        spread_q(f, fu, 1)
                    if c == 5:
                        spread_v(f, fu, 3)

            def shift(n, c):
                if not live(n, B):
                    return
                dve.wait_ge(scores_ready, n + 1)
                src = sc[c % 2][:, :, :, :].rearrange("p j g k -> p (j g) k")
                nc.vector.tensor_reduce(mx[:, c % 2, :], src, AX.X, ALU.max).then_inc(max_ready, 1)
                dve.wait_ge(max_ready, n + 1)
                wait(dve, turned, n - 3)
                nc.vector.tensor_tensor(sh[:, c % 4, :].rearrange("p (h k) -> p h k", k=T), src,
                                        mx[:, c % 2, :].unsqueeze(2).broadcast_to([P, NPAIR * G, T]), ALU.subtract)\
                    .then_inc(shifted, 1)

            def normalize(n, c, su, u):
                if not live(n, B):
                    return
                wait(dve, out_read, n - 1)
                dve.wait_ge(out_ready, n + 1)
                o = po_view(c // 2)
                for j in range(2):
                    r = slice(64 * j, 64 * j + 64)
                    nc.vector.reciprocal(rec[r, :, :], o[r, :, :, j, HD]).then_inc(recip_ready, 1)
                dve.wait_ge(recip_ready, n + 1)
                for j in range(2):
                    r = slice(64 * j, 64 * j + 64)
                    if cross:
                        if c == 1:
                            wait(dve, c2_turned, su - 1)
                        out = c2[r, u, c - 1:c + 1, :, :]
                    else:
                        out = m.ctx[r, :, :, bass.ds(n - 1, 2)].rearrange("p h d b -> p b h d")
                    nc.vector.tensor_tensor(out, o[r, :, :, j, 0:HD], rec[r, :, :].unsqueeze(3).broadcast_to([64, 2, H // 2, HD]),
                                            ALU.mult).then_inc(out_read, 1)

            def add_out(f, fu, c):
                if cross and c == 7 and live(f - 2, UNITS):
                    wait(dve, o_ready, f - 1)
                    wait(dve, x1_biased, f - 1)
                    row = m.x[:, bass.ds(f - 2, 1), :, :].rearrange("p o q n -> p (o q n)")
                    nc.vector.tensor_tensor(row, bank(7)[:, :], row, ALU.add).then_inc(o_added, 1)

            pair = [None]

            def unit(su, u):
                f, fu = su + 1, 1 - u
                for c in range(UB):
                    n = UB * su + c
                    front(f, fu, c)
                    shift(n, c)
                    if (c - 4) % 2 == 1:
                        normalize(n - 4, (c - 4) % 8, su if c >= 4 else su - 1, u if c >= 4 else fu)
                    add_out(f, fu, c)

            unit(-1, 1)
            unit(0, 0)
            unit(1, 1)
            with dve.Fori(1, UNITS // 2 - 1) as k:
                pair[0] = k
                unit(2 * k, 0)
                pair[0] = k + 1
                unit(2 * k + 1, 1)
            unit(UNITS - 2, 0)
            unit(UNITS - 1, 1)
            unit(UNITS, 0)


def routing(nc, a, m):
    with ExitStack() as stack:
        s = Memory(nc)
        stack.enter_context(s.ctx)
        stats_ready, moments_ready, guessed, refined, xn_ready = (s.sem("r_" + n) for n in ("stats_ready", "moments_ready", "guessed", "refined", "xn_ready"))
        xt_ready, xt_copied, xs_copied, logits_ready, logits_read = (s.sem(n) for n in ("xt_ready", "xt_copied", "xs_copied", "logits_ready", "logits_read"))
        exp_ready, counts_ready, counted, step = (s.sem(n) for n in ("exp_ready", "counts_ready", "counted", "step"))
        shifted_logits = s.sem("shifted_logits")
        ps_t = [s.ps(f"ps_t{i}", [P, UT * P]) for i in range(2)]
        ps_l = [s.ps(f"ps_l{i}", [P, UT, E]) for i in range(2)]
        ps_c = s.ps("ps_c", [P, 2, E * UNITS])
        xn = s.sb("r_xn", [P, 2, UT, D])
        xs = s.sb("r_xs", [P, 2, UT * P])
        stats = s.sb("r_stats", [P, UT, 6])
        moments = s.sb("r_moments", [P, UT, 2])
        rstd, veps, newton = (s.sb("r_" + n, [P, UT]) for n in ("rstd", "veps", "newton"))
        lg = s.sb("lg", [P, TILES, E])
        pr = s.sb("pr", [P, E, TILES])
        red = s.sb("red", [P, TILES])
        thr = s.sb("thr", [P, E])
        cand = s.sb("cand", [P, E])
        hit = s.sb("hit", [P, E, TILES])
        cnt = s.sb("cnt", [P, E])
        flag = s.sb("flag", [P, E])
        flagi = s.sb("flagi", [P, E], I32)
        above = s.sb("above", [P, E, TILES])
        tie = s.sb("tie", [P, E, TILES])
        tierow = s.sb("tierow", [P, E, UNITS], BF16)
        rank = s.sb("rank", [P, E, TILES])
        base = s.sb("base", [P, E, UNITS])
        want = s.sb("want", [P, E])
        maski = s.sb("r_maski", [P, E, TILES], I32)
        key = s.sb("key", [P, E, TILES])
        best = s.sb("best", [P, TILES])
        free = s.sb("free", [P, TILES], I32)
        taken = s.sb("taken", [P, TILES])
        block = stack.enter_context(nc.Block())

        @block.tensor
        def _(pe):
            def unit(i, u):
                pe.wait_ge(xn_ready, UT * (i + 1))
                wait(pe, xt_copied, i - 1)
                for t in range(UT):
                    last = nc.tensor.transpose(ps_t[u][:, P * t:P * t + P], xn[:, u, t, :], m.ident[:, :])
                last.then_inc(xt_ready, 1)
                pe.wait_ge(xt_copied, i + 1)
                wait(pe, logits_read, i - 1)
                for t in range(UT):
                    last = nc.tensor.matmul(ps_l[u][:, t, :], xs[:, u, P * t:P * t + P], m.wg[:, :], start=True, stop=True)
                last.then_inc(logits_ready, 1)
            unit(0, 0)
            unit(1, 1)
            with pe.Fori(1, UNITS // 2) as k:
                unit(2 * k, 0)
                unit(2 * k + 1, 1)
            pe.wait_ge(counts_ready, 1)
            nc.tensor.matmul(ps_c[:, 0, 0:E], m.ones[:, :], cnt[:, :], start=True, stop=True).then_inc(counted, 1)
            with pe.Fori(1, 31) as i:
                pe.wait_ge(counts_ready, i + 1)
                nc.tensor.matmul(ps_c[:, 0, 0:E], m.ones[:, :], cnt[:, :], start=True, stop=True).then_inc(counted, 1)
            pe.wait_ge(counts_ready, 32)
            rows = tierow[:, :, :].rearrange("p e h -> p (e h)")
            nc.tensor.matmul(ps_c[:, 0, :], m.beforeb[:, :], rows, start=True, stop=True)
            nc.tensor.matmul(ps_c[:, 1, :], m.onesb[:, :], rows, start=True, stop=True).then_inc(counted, 1)

        @block.scalar
        def _(act):
            def unit(i, u):
                act.wait_ge(xt_ready, i + 1)
                wait(act, logits_ready, i - 1)
                wait(act, xs_copied, i - 1)
                nc.scalar.activation(xs[:, u, :], ps_t[u][:, :], ACT.Copy).then_inc(xt_copied, 1)
            unit(0, 0)
            unit(1, 1)
            with act.Fori(1, UNITS // 2) as k:
                unit(2 * k, 0)
                unit(2 * k + 1, 1)
            act.wait_ge(shifted_logits, 1)
            nc.scalar.activation(lg[:, :, :], lg[:, :, :], ACT.Exp).then_inc(exp_ready, 1)

        @block.gpsimd
        def _(pool):
            def unit(i, u):
                refine_rstd(nc, pool, veps[:, :], rstd[:, :], newton[:, :], guessed, refined, i)
                pool.wait_ge(xt_copied, i + 1)
                nc.gpsimd.tensor_copy(m.x3t[:, bass.ds(i, 1), :].rearrange("p o n -> p (o n)"), xs[:, u, :]).then_inc(xs_copied, 1)
            unit(0, 0)
            unit(1, 1)
            with pool.Fori(1, UNITS // 2) as k:
                unit(2 * k, 0)
                unit(2 * k + 1, 1)

        @block.vector
        def _(dve):
            def unit(i, u):
                src = [m.x[:, bass.ds(i, 1), t, :].rearrange("p o n -> p (o n)") for t in range(UT)]
                for t in range(UT):
                    nc.vector.bn_stats(stats[:, t, :], src[t]).then_inc(stats_ready, 1)
                for t in range(UT):
                    wait_apart(dve, stats_ready, UT * i + t + 1)
                    nc.vector.bn_aggr(moments[:, t, :], stats[:, t, :]).then_inc(moments_ready, 1)
                guess_rstd(nc, dve, moments[:, :, 1], veps[:, :], rstd[:, :], moments_ready, guessed, i)
                dve.wait_ge(refined, 4 * NEWTON * (i + 1))
                wait(dve, xt_ready, i - 1)
                for t in range(UT):
                    nc.vector.tensor_scalar(xn[:, u, t, :], src[t], moments[:, t, 0:1], rstd[:, t:t + 1], ALU.subtract, ALU.mult)\
                        .then_inc(xn_ready, 1)
                if not known(i) or i > 0:
                    read_logits(i - 1, 1 - u)

            def read_logits(i, u):
                dve.wait_ge(logits_ready, i + 1)
                nc.vector.tensor_copy(lg[:, bass.ds(UT * i, UT), :], ps_l[u][:, :, :]).then_inc(logits_read, 1)

            unit(0, 0)
            unit(1, 1)
            with dve.Fori(1, UNITS // 2) as k:
                unit(2 * k, 0)
                unit(2 * k + 1, 1)
            read_logits(UNITS - 1, 1)
            dve.wait_ge(logits_read, UNITS)

            done = [0]

            def then(ins):
                done[0] += 1
                ins.then_inc(step, 1)
                dve.wait_ge(step, done[0])

            wide = lambda t: t.unsqueeze(2).broadcast_to([P, TILES, E])
            per_expert = lambda t: t[:, :].unsqueeze(2).broadcast_to([P, E, TILES])
            per_token = lambda t: t[:, :].unsqueeze(1).broadcast_to([P, E, TILES])
            then(nc.vector.tensor_reduce(red[:, :], lg[:, :, :], AX.X, ALU.max))
            nc.vector.tensor_tensor(lg[:, :, :], lg[:, :, :], wide(red[:, :]), ALU.subtract).then_inc(shifted_logits, 1)
            dve.wait_ge(exp_ready, 1)
            then(nc.vector.tensor_reduce(red[:, :], lg[:, :, :], AX.X, ALU.add))
            then(nc.vector.reciprocal(red[:, :], red[:, :]))
            then(nc.vector.tensor_tensor(pr[:, :, :].rearrange("p e t -> p t e"), lg[:, :, :], wide(red[:, :]), ALU.mult))
            then(nc.vector.memset(thr[:, :], 0.0))
            for bit in range(29, -1, -1):
                i = 29 - bit
                then(nc.vector.tensor_scalar(cand[:, :].bitcast(I32), thr[:, :].bitcast(I32), 1 << bit, None, ALU.bitwise_or))
                then(nc.vector.tensor_tensor(hit[:, :, :], pr[:, :, :], per_expert(cand), ALU.is_ge))
                nc.vector.tensor_reduce(cnt[:, :], hit[:, :, :], AX.X, ALU.add).then_inc(counts_ready, 1)
                dve.wait_ge(counted, i + 1)
                then(nc.vector.tensor_scalar(flagi[:, :], ps_c[:, 0, 0:E], float(CAP), None, ALU.is_ge))
                then(nc.vector.copy_predicated(thr[:, :], flagi[:, :], cand[:, :]))
            then(nc.vector.tensor_tensor(above[:, :, :], pr[:, :, :], per_expert(thr), ALU.is_gt))
            nc.vector.tensor_reduce(cnt[:, :], above[:, :, :], AX.X, ALU.add).then_inc(counts_ready, 1)
            dve.wait_ge(counted, 31)
            then(nc.vector.tensor_scalar(want[:, :], ps_c[:, 0, 0:E], -1.0, float(CAP), ALU.mult, ALU.add))
            then(nc.vector.tensor_tensor(tie[:, :, :], pr[:, :, :], per_expert(thr), ALU.is_equal))
            by_unit = lambda t: t[:, :, :].rearrange("p e (h q) -> p e h q", q=UT)
            then(nc.vector.tensor_reduce(base[:, :, :], by_unit(tie), AX.X, ALU.add))
            nc.vector.tensor_copy(tierow[:, :, :], base[:, :, :]).then_inc(counts_ready, 1)
            dve.wait_ge(counted, 32)
            in_unit = ps_c[:, 0, :].rearrange("p (e h) -> p e h", e=E)
            of_unit = ps_c[:, 1, :].rearrange("p (e h) -> p e h", e=E)
            then(nc.vector.memset(base[:, :, 0:1], 0.0))
            for h in range(1, UNITS):
                then(nc.vector.tensor_tensor(base[:, :, h], of_unit[:, :, h - 1], base[:, :, h - 1], ALU.add))
            then(nc.vector.tensor_tensor(base[:, :, :], in_unit, base[:, :, :], ALU.add))
            then(nc.vector.tensor_tensor(by_unit(rank)[:, :, :, 0], base[:, :, :], by_unit(tie)[:, :, :, 0], ALU.add))
            for q in range(1, UT):
                then(nc.vector.tensor_tensor(by_unit(rank)[:, :, :, q], by_unit(rank)[:, :, :, q - 1], by_unit(tie)[:, :, :, q], ALU.add))
            then(nc.vector.tensor_tensor(rank[:, :, :], rank[:, :, :], per_expert(want), ALU.is_le))
            then(nc.vector.tensor_tensor(tie[:, :, :], tie[:, :, :], rank[:, :, :], ALU.mult))
            then(nc.vector.tensor_tensor(maski[:, :, :], above[:, :, :], tie[:, :, :], ALU.add))
            then(nc.vector.memset(key[:, :, :], -1.0))
            then(nc.vector.copy_predicated(key[:, :, :], maski[:, :, :], pr[:, :, :]))
            then(nc.vector.tensor_reduce(best[:, :], key[:, :, :].rearrange("p e t -> p t e"), AX.X, ALU.max))
            then(nc.vector.tensor_scalar(free[:, :], best[:, :], 0.0, None, ALU.is_lt))
            for e in range(E):
                then(nc.vector.copy_predicated(key[:, e, :], free[:, :], pr[:, e, :]))
            then(nc.vector.tensor_reduce(best[:, :], key[:, :, :].rearrange("p e t -> p t e"), AX.X, ALU.max))
            then(nc.vector.tensor_tensor(hit[:, :, :], key[:, :, :], per_token(best), ALU.is_equal))
            then(nc.vector.memset(taken[:, :], 0.0))
            for e in range(E):
                then(nc.vector.tensor_tensor(red[:, :], hit[:, e, :], taken[:, :], ALU.is_gt))
                then(nc.vector.tensor_tensor(taken[:, :], taken[:, :], hit[:, e, :], ALU.max))
                then(nc.vector.tensor_tensor(m.gate[:, e, :], red[:, :], best[:, :], ALU.mult))


def experts(nc, a, m, out):
    with ExitStack() as stack:
        s = Memory(nc)
        stack.enter_context(s.ctx)
        w_loaded, h_ready, g_ready, y_ready, gated = (s.sem(n) for n in ("w_loaded", "h_ready", "g_ready", "yy_ready", "gated"))
        stored = s.sem("stored")
        ph = [s.ps(f"ph{i}", [P, 2, 512]) for i in range(2)]
        py = [s.ps(f"py{i}", [P, UT, D]) for i in range(2)]
        w1 = s.sb("w1", [P, E, FF])
        w2 = s.sb("w2", [P, E, 2, D])
        hh = s.sb("hh", [P, 2, 2, 512])
        block = stack.enter_context(nc.Block())

        @block.sync
        def _(sp):
            sp.dma_start(w1[:, :, :], a["w1"]).then_inc(w_loaded, 16)
            sp.dma_start(w2[:, :, :, :], a["w2"]).then_inc(w_loaded, 16)
            with sp.Fori(0, UNITS) as i:
                sp.wait_ge(gated, E * UT * (i + 1))
                sp.dma_start(out[bass.ds(i, 1)].rearrange("o b n -> (o b) n"), m.x[:, bass.ds(i, 1), :, :].rearrange("p o q n -> p (o q n)"))\
                    .then_inc(stored, 16)
            sp.wait_ge(stored, 16 * UNITS)

        @block.tensor
        def _(pe):
            pe.wait_ge(w_loaded, 32)

            def up(i, e):
                wait(pe, g_ready, 2 * (E * i + e) - 2)
                for f in range(2):
                    nc.tensor.matmul(ph[e % 2][:, f, :], w1[:, e, P * f:P * f + P], m.x3t[:, bass.ds(i, 1), :].rearrange("p o n -> p (o n)"),
                                     start=True, stop=True).then_inc(h_ready, 1)

            def down(i, e, n=0):
                wait(pe, g_ready, 2 * (E * i + e) + 2)
                wait(pe, gated, UT * (E * i + e - 1))
                for t in range(UT):
                    for f in range(2):
                        last = nc.tensor.matmul(py[e % 2][:, t, :], hh[:, e % 2, f, P * t:P * t + P], w2[:, e, f, :],
                                                start=(f == 0), stop=(f == 1))
                last.then_inc(y_ready, 1)

            def chunk(i):
                for e in range(E):
                    up(i, e)
                    if e or not known(i) or i > 0:
                        down(i - (e == 0), (e - 1) % E)
            chunk(0)
            with pe.Fori(1, UNITS) as i:
                chunk(i)
            down(UNITS - 1, E - 1)

        @block.scalar
        def _(act):
            def chunk(i):
                for e in range(E):
                    wait(act, y_ready, E * i + e - 1)
                    for f in range(2):
                        act.wait_ge(h_ready, 2 * (E * i + e) + f + 1)
                        nc.scalar.activation(hh[:, e % 2, f, :], ph[e % 2][:, f, :], ACT.Gelu).then_inc(g_ready, 1)
            chunk(0)
            with act.Fori(1, UNITS) as i:
                chunk(i)

        @block.vector
        def _(dve):
            def chunk(i):
                for e in range(E):
                    dve.wait_ge(y_ready, E * i + e + 1)
                    if not known(i) or i > 0 or e:
                        dve.wait_ge(gated, UT * (E * i + e))
                    for t in range(UT):
                        row = m.x[:, bass.ds(i, 1), t, :].rearrange("p o n -> p (o n)")
                        ins = nc.vector.scalar_tensor_tensor(out=row, in0=py[e % 2][:, t, :], scalar=m.gate[:, e, bass.ds(UT * i + t, 1)],
                                                             in1=row, op0=ALU.mult, op1=ALU.add)
                        ins.then_inc(gated, 1)
            chunk(0)
            with dve.Fori(1, UNITS) as i:
                chunk(i)


def decoder_layer(nc, a, out):
    m = Memory(nc)
    with m.ctx:
        m.ident = m.sb("ident", [P, P])
        m.qscale = m.sb("qscale", [P, C])
        m.dupf = m.sb("dupf", [P, P])
        m.dup = m.sb("dup", [P, P], BF16)
        m.before = m.sb("before", [P, P])
        m.beforeb = m.sb("beforeb", [P, P], BF16)
        m.ones = m.sb("ones", [P, P])
        m.onesb = m.sb("onesb", [P, P], BF16)
        m.wg = m.sb("wg", [P, E])
        m.tb = m.sb("tb", [P, T])
        m.gates = m.sb("gates", [P, 4])
        m.maski = m.sb("maski", [P, T], I32)
        m.maskf = m.sb("maskf", [P, T])
        m.maskb = m.sb("maskb", [P, T], BF16)
        m.tb_hi, m.tb_mid, m.tb_lo, m.tb_hm = (m.sb(n, [P, T], BF16) for n in ("tb_hi", "tb_mid", "tb_lo", "tb_hm"))
        m.tb_rest = m.sb("tb_rest", [P, T])
        m.bo_row = m.sb("bo_row", [P, 2, D])
        m.w2o = m.sb("w2o", [P, D])
        m.wqkv = m.sb("wqkv", [P, 2, 3, D])
        m.bqk = m.sb("bqk", [P, 2, 2])
        m.bv = m.sb("bv", [P, 2, UB * T])
        m.gate = m.sb("gate", [P, E, TILES])
        m.x = m.sb("x", [P, UNITS, UT, D])
        m.ctx_ = m.sb("ctx", [P, H // 2, HD, B])
        m.x3t = m.ctx_[:, :, :, :].rearrange("p h d b -> p (h d b)").rearrange("p (u n) -> p u n", u=UNITS)
        att = ExitStack()
        keep, m.ctx = m.ctx, att
        m.wexp = m.sb("wexp", [P, HD, 8 * D])
        m.qexp = m.sb("qexp", [P, 2, UB, C, T])
        m.kexp = m.sb("kexp", [P, 2, UB, G, T])
        m.vb = m.sb("vb", [P, 2, UB * 4, 2, 2, OW])
        m.ctx = m.ctx_
        setup(nc, a, m)
        attention(nc, a, m, False)
        attention(nc, a, m, True)
        att.close()
        routing(nc, a, m)
        experts(nc, a, m, out)
        m.ctx = keep


def kernel(**inputs):
    import numpy as np
    import concourse.bacc as bacc
    from concourse.bass_utils import run_bass_kernel_spmd

    w = {k: np.asarray(v) for k, v in inputs.items()}
    at, xa = "L0_attn_", "L0_xattn_"
    pos = np.arange(T)
    rows = np.stack([w[at + "time_bias"][0, 0, 250 - q:250 - q + T] for q in range(T)])
    mask = w["mask_1x1xSxS2_ik0"][0, 0]
    dup = (pos[:, None] == pos[None, :]).astype(np.float32)
    arrays = {
        "x_tiles": w["x"].reshape(UNITS, UT, P, D),
        "x_rows": w["x"].reshape(UNITS, P, UT * D),
        "ctx_tiles": w["ctx_1024"].reshape(UNITS, UT, P, D),
        "ident": np.eye(P, dtype=np.float32),
        "class_scale": ((np.arange(P)[:, None] % 32) // HD == np.arange(C)[None, :]).astype(np.float32) * np.float32(HD ** -0.5),
        "dup": np.tile(dup, (2, 2)),
        "before": (np.arange(P)[:, None] < np.arange(P)[None, :]).astype(np.float32),
        "wg": w["L0_ffn_Wg"],
        "time_tile": np.concatenate([rows, rows]),
        "et_gate": w[at + "et_gate"].reshape(1),
        "is_gate": w[at + "is_gate"].reshape(1),
        "mask_tile": np.concatenate([mask, mask]),
        "self_bo": w[at + "bo"],
        "cross_bo": w[xa + "bo"],
        "cross_wo": w[xa + "wo"].T.reshape(H // 2, 2, HD, D).transpose(1, 0, 2, 3).reshape(P, D),
        "self_wo": w[at + "Wo"].T.reshape(16, HD, D),
        "w1": w["L0_ffn_W1"].transpose(1, 0, 2),
        "w2": w["L0_ffn_W2"].reshape(E, 2, P, D).transpose(2, 0, 1, 3),
    }
    for who, p, up in (("self", at, True), ("cross", xa, False)):
        for x in "qkv":
            arrays[f"{who}_w{x}"] = w[p + ("W" if up else "w") + x].T
            b = w[p + "b" + x]
            arrays[f"{who}_b{x}"] = b.reshape(P, 1)
        arrays[f"{who}_bv"] = np.tile(b.reshape(G // 2, 2, C * HD).transpose(1, 0, 2).reshape(2, -1), (1, UB))
    arrays = {k: np.ascontiguousarray(v) for k, v in arrays.items()}
    nc = bacc.Bacc("TRN2", target_bir_lowering=False, num_devices=1)
    aps = {k: nc.dram_tensor(k + "_dram", v.shape, mybir.dt.from_np(v.dtype), kind="ExternalInput").ap() for k, v in arrays.items()}
    out = nc.dram_tensor("out_dram", (UNITS, P, UT * D), F32, kind="ExternalOutput").ap()
    decoder_layer(nc, aps, out)
    r = run_bass_kernel_spmd(nc, [{k + "_dram": v for k, v in arrays.items()}], core_ids=[0])
    return r.results[0]["out_dram"].reshape(B, T, D)
```

```python
from contextlib import ExitStack

import concourse.bass as bass
from concourse import mybir

F32 = mybir.dt.float32
BF16 = mybir.dt.bfloat16
I32 = mybir.dt.int32
ALU = mybir.AluOpType
ACT = mybir.ActivationFunctionType
AX = mybir.AxisListType

P = 128
B, T, D = 128, 64, 128
H, HD = 16, 8
C = P // 32
G = H // C
NPAIR = C // 2
UB = 8
UNITS = B // UB
UT = UB * T // P
SW = G * T
OW = HD + 1
OB = H * OW
E, FF = 8, 256
TILES = B * T // P
CAP = B * T // E
NT = TILES + E
ROW = D + 4
MEAN, RSTD, WEIGHT, INDEX = range(D, ROW)
BITS = 30
RING = 8
EPS = 1e-5
MASKED = -1e30


def known(v):
    return isinstance(v, int)


def wait(eng, sem, value):
    if not known(value) or value > 0:
        eng.wait_ge(sem, value)


def wait_apart(eng, sem, value):
    wait(eng, sem, value)
    if not known(value):
        eng.nop(nofuse=True)


def at_most(value, most):
    return min(value, most) if known(value) else value


def live(n, count):
    return not known(n) or 0 <= n < count


def units(eng, unit):
    unit(-1, 1)
    unit(0, 0)
    unit(1, 1)
    with eng.Fori(1, UNITS // 2 - 1) as k:
        unit(2 * k, 0)
        unit(2 * k + 1, 1)
    unit(UNITS - 2, 0)
    unit(UNITS - 1, 1)
    unit(UNITS, 0)
    unit(UNITS + 1, 1)


NEWTON = 3


def guess_rstd(nc, dve, var, veps, guess, moments_ready, guessed, i):
    dve.wait_ge(moments_ready, UT * (i + 1))
    nc.vector.tensor_scalar(veps, var, EPS, None, ALU.add).then_inc(guessed, 1)
    dve.wait_ge(guessed, 3 * i + 1)
    nc.vector.tensor_scalar(guess.bitcast(I32), veps.bitcast(I32), 1, None, ALU.arith_shift_right).then_inc(guessed, 1)
    dve.wait_ge(guessed, 3 * i + 2)
    nc.vector.tensor_scalar(guess.bitcast(I32), guess.bitcast(I32), -1.0, float(0x5F3759DF), ALU.mult, ALU.add).then_inc(guessed, 1)


def refine_rstd(nc, pool, veps, y, t, guessed, refined, i):
    wait_apart(pool, guessed, 3 * i + 3)
    for k in range(NEWTON):
        done = 4 * NEWTON * i + 4 * k
        if k:
            wait_apart(pool, refined, done)
        nc.gpsimd.tensor_tensor(t, y, y, ALU.mult).then_inc(refined, 1)
        wait_apart(pool, refined, done + 1)
        nc.gpsimd.tensor_tensor(t, t, veps, ALU.mult).then_inc(refined, 1)
        wait_apart(pool, refined, done + 2)
        nc.gpsimd.tensor_scalar(t, t, -0.5, 1.5, ALU.mult, ALU.add).then_inc(refined, 1)
        wait_apart(pool, refined, done + 3)
        nc.gpsimd.tensor_tensor(y, y, t, ALU.mult).then_inc(refined, 1)


def x_of(m, i):
    return m.x[:, bass.ds(i, 1), :, :].rearrange("p o q n -> p (o q) n")


class Memory:

    def __init__(self, nc):
        self.nc = nc
        self.ctx = ExitStack()

    def sb(self, name, shape, dt=F32):
        return self.ctx.enter_context(self.nc.sbuf_tensor(name, shape, dt))

    def ps(self, name, shape, dt=F32):
        return self.ctx.enter_context(self.nc.psum_tensor(name, shape, dt))

    def sem(self, name):
        return self.ctx.enter_context(self.nc.semaphore(name))


def setup(nc, a, m):
    with ExitStack() as stack:
        s = Memory(nc)
        stack.enter_context(s.ctx)
        loaded, zeroed, padded, filled = (s.sem(n) for n in ("loaded", "zeroed", "padded", "filled"))
        gate, table, tmask, parts = (s.sem(n) for n in ("gate_ready", "table_ready", "mask_ready", "parts_ready"))
        block = stack.enter_context(nc.Block())
        loads = [
            (m.ident[:, :], a["ident"]),
            (m.qscale[:, :], a["class_scale"]),
            (m.dupf[:, :], a["dup"]),
            (m.before[:, :], a["before"]),
            (m.wg[:, :], a["wg"]),
            (m.tb[:, :], a["time_tile"]),
            (m.gates[:, 0:1], a["et_gate"].partition_broadcast(P)),
            (m.gates[:, 1:2], a["is_gate"].partition_broadcast(P)),
            (m.maski[:, :], a["mask_tile"]),
            (m.bo_row[:, 0, :], a["self_bo"].partition_broadcast(P)),
            (m.bo_row[:, 1, :], a["cross_bo"].partition_broadcast(P)),
            (m.wo[:, 0, :], a["self_wo"]),
            (m.wo[:, 1, :], a["cross_wo"]),
        ]
        for n, who in enumerate(("self", "cross")):
            loads += [(m.wqkv[:, n, w, :], a[f"{who}_w{x}"]) for w, x in enumerate("qkv")]
            loads += [(m.bqk[:, n, w:w + 1], a[f"{who}_b{x}"]) for w, x in enumerate("qk")]
            loads += [(m.bv[64 * gh:64 * gh + 64, n, :], a[f"{who}_bv"][gh].partition_broadcast(64)) for gh in range(2)]

        @block.sync
        def _(sp):
            for out, in_ in loads:
                sp.dma_start(out, in_).then_inc(loaded, 16)
            sp.wait_ge(padded, 2)
            sp.dma_start(m.sorted.rearrange("(t p) n -> p t n", p=P), m.pad[:, :].unsqueeze(1).broadcast_to([P, NT, ROW])).then_inc(filled, 16)
            sp.wait_ge(loaded, 16 * len(loads))
            sp.wait_ge(filled, 16)

        @block.gpsimd
        def _(pool):
            nc.gpsimd.memset(m.pad[:, 0:INDEX], 0.0).then_inc(padded, 1)
            nc.gpsimd.memset(m.pad[:, INDEX:ROW].bitcast(I32), B * T).then_inc(padded, 1)
            nc.gpsimd.memset(m.kexp[:, :, :, :, :], 0.0).then_inc(zeroed, 1)
            nc.gpsimd.memset(m.vb[:, :, :, :, :, :], 0.0).then_inc(zeroed, 1)
            pool.wait_ge(zeroed, 2)
            for gh in range(2):
                nc.gpsimd.memset(m.vb[64 * gh:64 * gh + 64, :, :, :, gh, HD:OW], 1.0).then_inc(zeroed, 1)

        @block.scalar
        def _(act):
            act.wait_ge(loaded, 16 * len(loads))
            nc.scalar.activation(m.gates[:, 2:3], m.gates[:, 0:1], ACT.Sigmoid).then_inc(gate, 1)

        @block.vector
        def _(dve):
            dve.wait_ge(loaded, 16 * len(loads))
            nc.vector.tensor_copy(m.dup[:, :], m.dupf[:, :])
            nc.vector.memset(m.ones[:, :], 1.0)
            nc.vector.memset(m.onesb[:, :], 1.0)
            nc.vector.tensor_copy(m.beforeb[:, :], m.before[:, :])
            nc.vector.tensor_copy(m.maskf[:, :], m.maski[:, :]).then_inc(tmask, 1)
            dve.wait_ge(tmask, 1)
            nc.vector.tensor_scalar(m.maskb[:, :], m.maskf[:, :], 0.0, MASKED, ALU.is_equal, ALU.mult).then_inc(tmask, 1)
            dve.wait_ge(gate, 1)
            nc.vector.tensor_scalar(m.tb[:, :], m.tb[:, :], m.gates[:, 2:3], m.gates[:, 1:2], ALU.mult, ALU.add).then_inc(table, 1)
            dve.wait_ge(table, 1)
            nc.vector.tensor_copy(m.tb_hi[:, :], m.tb[:, :]).then_inc(parts, 1)
            dve.wait_ge(parts, 1)
            nc.vector.tensor_tensor(m.tb_rest[:, :], m.tb[:, :], m.tb_hi[:, :], ALU.subtract).then_inc(parts, 1)
            dve.wait_ge(parts, 2)
            nc.vector.tensor_copy(m.tb_mid[:, :], m.tb_rest[:, :]).then_inc(parts, 1)
            dve.wait_ge(parts, 3)
            nc.vector.tensor_tensor(m.tb_lo[:, :], m.tb_rest[:, :], m.tb_mid[:, :], ALU.subtract).then_inc(parts, 1)
            nc.vector.tensor_copy(m.tb_hm[0:64, :], m.tb_hi[0:64, :]).then_inc(parts, 1)
            nc.vector.tensor_copy(m.tb_hm[64:128, :], m.tb_mid[64:128, :]).then_inc(parts, 1)
            dve.wait_ge(parts, 6)


def attention(nc, a, m, cross):
    n_att = 1 if cross else 0
    pre = "cross_" if cross else "self_"
    with ExitStack() as stack:
        s = Memory(nc)
        stack.enter_context(s.ctx)
        sem = lambda name: s.sem(pre + name)
        scores_ready, max_ready, shifted = sem("scores_ready"), sem("max_ready"), sem("shifted")
        probs_ready, turned, turned_copied = sem("probs_ready"), sem("turned"), sem("turned_copied")
        out_ready, recip_ready, out_read = sem("out_ready"), sem("recip_ready"), sem("out_read")
        x_loaded = [sem(f"x_loaded{u}") for u in range(2)]
        stats_ready, moments_ready, guessed, xn_ready = (sem(n) for n in ("stats_ready", "moments_ready", "guessed", "xn_ready"))
        refined = sem("refined")
        xt_ready, xt_copied = sem("xt_ready"), sem("xt_copied")
        q_done, q_ready, k_done, k_ready, v_done, v_ready = (sem(n) for n in ("q_done", "q_ready", "k_done", "k_ready", "v_done", "v_ready"))
        if cross:
            c_loaded = [sem(f"c_loaded{u}") for u in range(2)]
            y_copied, y_ready, x_biased, x1_ready, x1_biased = (sem(n) for n in ("y_copied", "y_ready", "x_biased", "x1_ready", "x1_biased"))
            ct_ready, ct_copied, c2_turned, c2_copied, o_ready, o_added = (sem(n) for n in ("ct_ready", "ct_copied", "c2_turned", "c2_copied", "o_ready", "o_added"))

        sc = [s.ps(f"{pre}sc{i}", [P, NPAIR, G, T]) for i in range(2)]
        pt = [s.ps(f"{pre}pt{i}", [P, 4, P]) for i in range(2)]
        po = [s.ps(f"{pre}po{i}", [P, 512]) for i in range(2)]
        job = [s.ps(f"{pre}job{i}", [P, 512]) for i in range(2)]
        xin = s.sb(pre + "xin", [P, 2, UT, D])
        xn = s.sb(pre + "xn", [P, UT, D])
        xnt = s.sb(pre + "xnt", [P, UT * P])
        stats = s.sb(pre + "stats", [P, UT, 6])
        moments = s.sb(pre + "moments", [P, UT, 2])
        rstd, veps, newton = (s.sb(pre + n, [P, UT]) for n in ("rstd", "veps", "newton"))
        mx = s.sb(pre + "mx", [P, 2, NPAIR * G])
        sh = s.sb(pre + "sh", [P, 4, NPAIR * G * T])
        pts = s.sb(pre + "pts", [P, 2, 4, P])
        rec = s.sb(pre + "rec", [P, 2, H // 2, 2])
        if cross:
            cin = s.sb(pre + "cin", [P, 2, UT, D])
            ct = s.sb(pre + "ct", [P, UT * P])
            yctx = s.sb(pre + "yctx", [P, UT, B])
            ctx_moved = sem("ctx_moved")
            stats2 = s.sb(pre + "stats2", [P, UT, 6])
            moments2 = s.sb(pre + "moments2", [P, UT, 2])
            rstd2, veps2, newton2 = (s.sb(pre + n, [P, UT]) for n in ("rstd2", "veps2", "newton2"))
            xn2 = s.sb(pre + "xn2", [P, UT, D])
            xn2t = s.sb(pre + "xn2t", [P, UT * P])
            stats2_ready, moments2_ready, guessed2, refined2, xn2_ready = (
                sem(n) for n in ("stats2_ready", "moments2_ready", "guessed2", "refined2", "xn2_ready"))
            xn2_turned, xn2_copied, logits_ready, logits_read, kept = (
                sem(n) for n in ("xn2_turned", "xn2_copied", "logits_ready", "logits_read", "kept"))
            c2 = s.sb(pre + "c2", [P, 2, UB, H // 2, HD])
            c2t = s.sb(pre + "c2t", [P, UB // 2, 2, T])
        kvt = ct if cross else xnt
        wq, wk, wv = (m.wqkv[:, n_att, w, :] for w in range(3))
        block = stack.enter_context(nc.Block())

        def po_view(pair):
            return po[pair % 2][:, 0:2 * OB].rearrange("p (b h j w) -> p b h j w", b=2, h=H // 2, j=2)

        def bank(j):
            return job[j % 2]

        @block.sync
        def _(sp):
            if cross:
                for d in range(HD):
                    for j in range(2):
                        for q in range(UT):
                            rows = 64 * j + 16 * q
                            sp.dma_start(m.ctxt[d:P:HD, j:H:2, q, :], m.ctx[rows:rows + 16, :, d, :]).then_inc(ctx_moved, 16)

            def unit(su, u):
                f, fu = su + 1, 1 - u
                if not live(f, UNITS):
                    return
                if cross:
                    wait(sp, x1_ready, f - 1)
                    sp.dma_start(xin[:, fu, :, :], a["x_rows"][bass.ds(f, 1)].rearrange("o b n -> (o b) n")
                                 .rearrange("b (q n) -> b q n", q=UT)).then_inc(x_loaded[fu], 16)
                    wait(sp, ct_ready, f - 1)
                    sp.dma_start(cin[:, fu, :, :], a["ctx_tiles"][bass.ds(f, 1)].rearrange("o t p n -> (o p) t n"))\
                        .then_inc(c_loaded[fu], 16)
                else:
                    wait(sp, xn_ready, UT * (f - 1))
                    sp.dma_start(xin[:, fu, :, :], a["x_tiles"][bass.ds(f, 1)].rearrange("o t p n -> (o p) t n"))\
                        .then_inc(x_loaded[fu], 16)
            units(sp, unit)

        @block.gpsimd
        def _(pool):
            def unit(su, u):
                f, fu = su + 1, 1 - u
                if not cross:
                    if live(f, UNITS):
                        refine_rstd(nc, pool, veps[:, :], rstd[:, :], newton[:, :], guessed, refined, f)
                    return
                if live(f, UNITS):
                    if known(f) and f == 0:
                        pool.wait_ge(ctx_moved, 16 * 8 * HD)
                        move_ctx(0)
                    pool.wait_ge(x_loaded[fu], 16 * (pair_of(f) + 1))
                    nc.gpsimd.tensor_tensor(xin[:, fu, :, :], xin[:, fu, :, :], bo_tiles(0), ALU.add).then_inc(x_biased, 1)
                z = f - 3
                if live(z, UNITS):
                    refine_rstd(nc, pool, veps2[:, :], rstd2[:, :], newton2[:, :], guessed2, refined2, z)
                    wait_apart(pool, refined2, 4 * NEWTON * (z + 1))
                    for src, col in ((moments2[:, :, 0], MEAN), (rstd2[:, :], RSTD)):
                        nc.gpsimd.tensor_copy(m.rows[:, bass.ds(z, 1), :, col].rearrange("p o q -> p (o q)"), src).then_inc(kept, 1)
                if live(f, UNITS):
                    refine_rstd(nc, pool, veps[:, :], rstd[:, :], newton[:, :], guessed, refined, f)
                    pool.wait_ge(xn_ready, UT * (f + 1))
                    nc.gpsimd.tensor_tensor(x_of(m, f), x_of(m, f), bo_tiles(1), ALU.add).then_inc(x1_biased, 1)
                if live(f + 1, UNITS):
                    move_ctx(f + 1)

            def move_ctx(f):
                wait(pool, y_ready, f)
                nc.gpsimd.tensor_copy(yctx[:, :, :], m.ctxt[:, bass.ds(f, 1), :, :].rearrange("p o q b -> p (o q) b"))\
                    .then_inc(y_copied, 1)

            def bo_tiles(n):
                return m.bo_row[:, n, :].unsqueeze(1).broadcast_to([P, UT, D])

            def pair_of(f):
                if known(f):
                    return f // 2
                return pairs[0]

            pairs = [None]

            unit(-1, 1)
            unit(0, 0)
            unit(1, 1)
            with pool.Fori(1, UNITS // 2 - 1) as k:
                pairs[0] = k
                unit(2 * k, 0)
                pairs[0] = k + 1
                unit(2 * k + 1, 1)
            unit(UNITS - 2, 0)
            unit(UNITS - 1, 1)
            unit(UNITS, 0)
            unit(UNITS + 1, 1)

        @block.tensor
        def _(pe):
            def scores(n, c, su, u):
                if not live(n, B):
                    return
                wait(pe, shifted, n - 1)
                if c == 0:
                    wait(pe, q_ready, su + 1)
                    wait(pe, k_ready, G * (su + 1))
                for jj in range(NPAIR):
                    out = sc[c % 2][:, jj, :, :]
                    nc.tensor.matmul(out, m.qexp[:, u, c, 2 * jj:2 * jj + 2, :], m.kexp[:, u, c, :, :], start=True, stop=False)
                    if cross:
                        last = nc.tensor.matmul(out, m.dup[0:64, :], m.maskb[0:64, :].unsqueeze(1).broadcast_to([64, G, T]),
                                                start=False, stop=True)
                    else:
                        nc.tensor.matmul(out, m.dup[:, :], m.tb_hm[:, :].unsqueeze(1).broadcast_to([P, G, T]), start=False, stop=False)
                        last = nc.tensor.matmul(out, m.dup[0:64, :], m.tb_lo[0:64, :].unsqueeze(1).broadcast_to([64, G, T]),
                                                start=False, stop=True)
                last.then_inc(scores_ready, 1)

            def turn(n, c):
                if not live(n, B):
                    return
                wait(pe, probs_ready, n + 1)
                wait(pe, turned_copied, n - 1)
                for i in range(4):
                    last = nc.tensor.transpose(pt[c % 2][:, i, :], sh[:, c % 4, P * i:P * i + P], m.ident[:, :])
                last.then_inc(turned, 1)

            def values(n, c, u, su):
                if not live(n, B):
                    return
                wait(pe, turned_copied, n + 1)
                if c == 0:
                    wait(pe, v_ready, 2 * (su + 1))
                if c % 2 == 0:
                    wait(pe, out_read, n - 2)
                o = po_view(c // 2)
                for jj in range(NPAIR):
                    for gp in range(G // 2):
                        out = o[:, c % 2, 4 * gp + jj:4 * gp + jj + 3:2, :, :].rearrange("p g j w -> p j g w")
                        last = nc.tensor.matmul(out, pts[:, c % 2, 2 * jj + gp, :], m.vb[:, u, 4 * c + 2 * gp + jj, :, :, :],
                                                start=True, stop=True)
                last.then_inc(out_ready, 1)

            def turn_tiles(out, tiles, sem_):
                for t in range(UT):
                    last = nc.tensor.transpose(out[:, P * t:P * t + P], tiles[:, t, :], m.ident[:, :])
                last.then_inc(sem_, 1)

            def turn_x(f, fu, j):
                pe.wait_ge(xn_ready, UT * (f + 1))
                turn_tiles(bank(j), xn, xt_ready)

            def project_q(f, fu, j):
                pe.wait_ge(xt_copied, f + 1)
                nc.tensor.matmul(bank(j)[:, :], wq, xnt[:, :], start=True, stop=True).then_inc(q_done, 1)

            def project_k(f, fu, j):
                pe.wait_ge(ct_copied if cross else xt_copied, f + 1)
                if cross:
                    pe.wait_ge(xt_copied, f + 1)
                nc.tensor.matmul(bank(j)[:, :], wk, kvt[:, :], start=True, stop=True).then_inc(k_done, 1)

            def project_v(f, fu, j):
                pe.wait_ge(q_ready, f + 1)
                for gh in range(2):
                    w = wv.rearrange("p (gp g c) -> p gp g c", g=2, c=C * HD)[:, :, gh, :]
                    for b in range(UB):
                        last = nc.tensor.matmul(bank(j)[64 * gh:64 * gh + 64, T * b:T * b + T].rearrange("p (g c) -> p g c", g=G // 2),
                                                kvt[:, T * b:T * b + T], w, start=True, stop=True)
                last.then_inc(v_done, 1)

            def self_front(f, fu, c):
                if not live(f, UNITS):
                    return
                if c == 2:
                    wait(pe, k_ready, G * f)
                    turn_x(f, fu, 0)
                if c == 3:
                    wait(pe, v_ready, 2 * f)
                    project_q(f, fu, 1)
                if c == 4:
                    project_k(f, fu, 2)
                if c == 5:
                    project_v(f, fu, 3)

            def cross_front(f, fu, c):
                if live(f, UNITS):
                    if c == 0:
                        wait(pe, k_ready, G * f)
                        wait(pe, c2_copied, 4 * (f - 2))
                        pe.wait_ge(y_copied, f + 1)
                        for q in range(UT):
                            last = nc.tensor.matmul(bank(0)[:, D * q:D * q + D], yctx[:, q, :], m.wo[:, 0, :], start=True, stop=True)
                        last.then_inc(y_ready, 1)
                    if c == 1:
                        wait(pe, v_ready, 2 * f)
                        wait(pe, o_added, f - 2)
                        pe.wait_ge(c_loaded[fu], 16 * ((f // 2 if known(f) else pair[0]) + 1))
                        turn_tiles(bank(1), cin[:, fu, :, :], ct_ready)
                    if c == 3:
                        turn_x(f, fu, 2)
                    if c == 4:
                        project_q(f, fu, 3)
                        project_k(f, fu, 4)
                    if c == 5:
                        project_v(f, fu, 5)
                z = f - 3
                if live(z, UNITS):
                    if c == 5:
                        wait(pe, k_ready, at_most(G * (f + 1), G * UNITS))
                        wait(pe, c2_copied, at_most(4 * (f - 2), 4 * UNITS))
                        wait(pe, xn2_ready, UT * (z + 1))
                        turn_tiles(bank(6), xn2, xn2_turned)
                    if c == 6:
                        wait(pe, v_ready, at_most(2 * (f + 1), 2 * UNITS))
                        wait(pe, o_added, at_most(f - 2, UNITS))
                        wait(pe, xn2_copied, z + 1)
                        for t in range(UT):
                            last = nc.tensor.matmul(bank(7)[:, E * t:E * t + E], xn2t[:, P * t:P * t + P], m.wg[:, :], start=True, stop=True)
                        last.then_inc(logits_ready, 1)
                if live(f - 2, UNITS):
                    if c == 6:
                        wait(pe, xn2_copied, z + 1)
                        wait(pe, k_ready, at_most(G * (f + 1), G * UNITS))
                        wait(pe, out_read, 8 * (f - 1))
                        wait(pe, c2_copied, 4 * (f - 2))
                        for t in range(UB // 2):
                            last = nc.tensor.transpose(bank(6)[:, P * t:P * t + P],
                                                       c2[:, fu, 2 * t:2 * t + 2, :, :].rearrange("p b h d -> p (b h d)"), m.ident[:, :])
                        last.then_inc(c2_turned, 1)
                    if c == 7:
                        wait(pe, logits_read, z + 1)
                        wait(pe, v_ready, at_most(2 * (f + 1), 2 * UNITS))
                        wait(pe, o_added, f - 2)
                        wait(pe, c2_copied, 4 * (f - 1))
                        tok = c2t[:, :, :, :].rearrange("p b c (t q) -> p q (b c t)", q=UT)
                        for q in range(UT):
                            last = nc.tensor.matmul(bank(7)[:, D * q:D * q + D], tok[:, q, :], m.wo[:, 1, :],
                                                    start=True, stop=True)
                        last.then_inc(o_ready, 1)

            pair = [None]

            def unit(su, u):
                f, fu = su + 1, 1 - u
                for c in range(UB):
                    n = UB * su + c
                    scores(n, c, su, u)
                    turn(n - 2, (c - 2) % 8)
                    c3 = (c - 3) % 8
                    values(n - 3, c3, u if c >= 3 else fu, su if c >= 3 else su - 1)
                    (cross_front if cross else self_front)(f, fu, c)

            unit(-1, 1)
            unit(0, 0)
            unit(1, 1)
            with pe.Fori(1, UNITS // 2 - 1) as k:
                pair[0] = k
                unit(2 * k, 0)
                pair[0] = k + 1
                unit(2 * k + 1, 1)
            unit(UNITS - 2, 0)
            unit(UNITS - 1, 1)
            unit(UNITS, 0)
            unit(UNITS + 1, 1)

        @block.scalar
        def _(act):
            def unit(su, u):
                f, fu = su + 1, 1 - u
                for c in range(UB):
                    n = UB * su + c
                    if live(f, UNITS):
                        if cross and c == 2:
                            act.wait_ge(ct_ready, f + 1)
                            nc.scalar.activation(ct[:, :], bank(1)[:, :], ACT.Copy).then_inc(ct_copied, 1)
                        if c == (4 if cross else 3):
                            act.wait_ge(xt_ready, f + 1)
                            if cross:
                                nc.scalar.activation(xnt[:, :].rearrange("p (b q) -> p q b", q=UT),
                                                     bank(2)[:, :].rearrange("p (q b) -> p q b", q=UT), ACT.Copy).then_inc(xt_copied, 1)
                            else:
                                nc.scalar.activation(xnt[:, :], bank(0)[:, :], ACT.Copy).then_inc(xt_copied, 1)
                        if c == 5:
                            act.wait_ge(k_done, f + 1)
                            for g in range(G):
                                r = slice(32 * g, 32 * g + 32)
                                nc.scalar.activation(m.kexp[r, fu, :, g, :],
                                                     bank(4 if cross else 2)[r, :].rearrange("p (b k) -> p b k", b=UB),
                                                     ACT.Identity, bias=m.bqk[r, n_att, 1:2]).then_inc(k_ready, 1)
                    if cross and c == 6 and live(f - 3, UNITS):
                        wait(act, xn2_turned, f - 2)
                        wait(act, logits_ready, f - 3)
                        nc.scalar.activation(xn2t[:, :], bank(6)[:, :], ACT.Copy).then_inc(xn2_copied, 1)
                    if cross and c == 7 and live(f - 2, UNITS):
                        wait(act, c2_turned, f - 1)
                        wait(act, o_ready, f - 2)
                        for j in range(2):
                            for bp in range(2):
                                nc.scalar.activation(c2t[64 * j:64 * j + 64, :, bp, :],
                                                     bank(6)[64 * bp:64 * bp + 64, :].rearrange(
                                                         "p (b j q) -> p b j q", j=2, q=T)[:, :, j, :],
                                                     ACT.Copy).then_inc(c2_copied, 1)
                    if live(n - 2, B):
                        wait(act, turned, n - 1)
                        wait(act, out_ready, n - 3)
                        nc.scalar.activation(pts[:, c % 2, :, :], pt[c % 2][:, :, :], ACT.Copy).then_inc(turned_copied, 1)
                    if live(n, B):
                        wait(act, shifted, n + 1)
                        nc.scalar.activation(sh[:, c % 4, :], sh[:, c % 4, :], ACT.Exp).then_inc(probs_ready, 1)
            units(act, unit)

        @block.vector
        def _(dve):
            def x_tiles(f, fu):
                if cross:
                    return [x_of(m, f)[:, t, :] for t in range(UT)]
                return [xin[:, fu, t, :] for t in range(UT)]

            def moments_x(f, fu):
                src = x_tiles(f, fu)
                for t in range(UT):
                    nc.vector.bn_stats(stats[:, t, :], src[t]).then_inc(stats_ready, 1)
                for t in range(UT):
                    wait_apart(dve, stats_ready, UT * f + t + 1)
                    nc.vector.bn_aggr(moments[:, t, :], stats[:, t, :]).then_inc(moments_ready, 1)
                guess_rstd(nc, dve, moments[:, :, 1], veps[:, :], rstd[:, :], moments_ready, guessed, f)

            def norm_x(f, fu):
                dve.wait_ge(refined, 4 * NEWTON * (f + 1))
                wait(dve, xt_ready, f)
                src = x_tiles(f, fu)
                for t in range(UT):
                    nc.vector.tensor_scalar(xn[:, t, :], src[t], moments[:, t, 0:1], rstd[:, t:t + 1], ALU.subtract, ALU.mult)\
                        .then_inc(xn_ready, 1)

            def spread_q(f, fu, j):
                dve.wait_ge(q_done, f + 1)
                for c in range(C):
                    nc.vector.tensor_scalar(m.qexp[:, fu, :, c, :], bank(j)[:, :].rearrange("p (b q) -> p b q", b=UB),
                                            m.bqk[:, n_att, 0:1], m.qscale[:, c:c + 1], ALU.add, ALU.mult)\
                        .then_inc(*((q_ready, 1) if c == C - 1 else (q_part, 1)))

            q_part = sem("q_part")

            def spread_v(f, fu, j):
                dve.wait_ge(v_done, f + 1)
                for gh in range(2):
                    r = slice(64 * gh, 64 * gh + 64)
                    view = lambda t: t.rearrange("p (x c d) -> p x c d", c=C, d=HD)
                    out = m.vb[r, fu, :, :, gh, 0:HD].rearrange("p (x j) c d -> p x (j c) d", j=NPAIR)
                    nc.vector.tensor_tensor(out, view(bank(j)[r, :]), view(m.bv[r, n_att, :]), ALU.add).then_inc(v_ready, 1)

            def late(f, c):
                z = f - 3
                if not cross or not live(z, UNITS):
                    return
                if c == 0:
                    wait_apart(dve, o_added, z + 1)
                    for t in range(UT):
                        nc.vector.bn_stats(stats2[:, t, :], x_of(m, z)[:, t, :]).then_inc(stats2_ready, 1)
                    wait(dve, kept, 2 * z)
                    for t in range(UT):
                        wait_apart(dve, stats2_ready, UT * z + t + 1)
                        nc.vector.bn_aggr(moments2[:, t, :], stats2[:, t, :]).then_inc(moments2_ready, 1)
                    guess_rstd(nc, dve, moments2[:, :, 1], veps2[:, :], rstd2[:, :], moments2_ready, guessed2, z)
                if c == 3:
                    wait(dve, refined2, 4 * NEWTON * (z + 1))
                    wait(dve, xn2_turned, z)
                    for t in range(UT):
                        nc.vector.tensor_scalar(xn2[:, t, :], x_of(m, z)[:, t, :], moments2[:, t, 0:1], rstd2[:, t:t + 1],
                                                ALU.subtract, ALU.mult).then_inc(xn2_ready, 1)
                if c == 7:
                    wait_apart(dve, logits_ready, z + 1)
                    nc.vector.tensor_copy(m.lg[:, bass.ds(UT * z, UT), :], bank(7)[:, 0:UT * E].rearrange("p (t e) -> p t e", e=E))\
                        .then_inc(logits_read, 1)

            def front(f, fu, c):
                if not live(f, UNITS):
                    return
                if cross:
                    if c == 1:
                        dve.wait_ge(y_ready, f + 1)
                        dve.wait_ge(x_biased, f + 1)
                        nc.vector.tensor_tensor(x_of(m, f), bank(0)[:, :].rearrange("p (q n) -> p q n", q=UT), xin[:, fu, :, :], ALU.add).then_inc(x1_ready, 1)
                        wait_apart(dve, x1_ready, f + 1)
                        moments_x(f, fu)
                    if c == 3:
                        norm_x(f, fu)
                    if c == 5:
                        spread_q(f, fu, 3)
                    if c == 6:
                        spread_v(f, fu, 5)
                else:
                    if c == 0:
                        dve.wait_ge(x_loaded[fu], 16 * (f // 2 + 1 if known(f) else pair[0] + 1))
                        moments_x(f, fu)
                    if c == 2:
                        norm_x(f, fu)
                    if c == 4:
                        spread_q(f, fu, 1)
                    if c == 6:
                        spread_v(f, fu, 3)

            def shift(n, c):
                if not live(n, B):
                    return
                dve.wait_ge(scores_ready, n + 1)
                src = sc[c % 2][:, :, :, :].rearrange("p j g k -> p (j g) k")
                nc.vector.tensor_reduce(mx[:, c % 2, :], src, AX.X, ALU.max).then_inc(max_ready, 1)
                dve.wait_ge(max_ready, n + 1)
                wait(dve, turned, n - 3)
                nc.vector.tensor_tensor(sh[:, c % 4, :].rearrange("p (h k) -> p h k", k=T), src,
                                        mx[:, c % 2, :].unsqueeze(2).broadcast_to([P, NPAIR * G, T]), ALU.subtract)\
                    .then_inc(shifted, 1)

            def normalize(n, c, su, u):
                if not live(n, B):
                    return
                pairs_done = 4 * su + (c + 1) // 2
                wait(dve, out_read, n - 1)
                dve.wait_ge(out_ready, n + 1)
                o = po_view(c // 2)
                nc.vector.reciprocal(rec[:, :, :, :], o[:, :, :, :, HD]).then_inc(recip_ready, 1)
                dve.wait_ge(recip_ready, pairs_done)
                for j in range(2):
                    r = slice(64 * j, 64 * j + 64)
                    if cross:
                        if c == 1:
                            wait(dve, c2_turned, su - 1)
                        out = c2[r, u, c - 1:c + 1, :, :]
                    else:
                        out = m.ctx[r, :, :, bass.ds(n - 1, 2)].rearrange("p h d b -> p b h d")
                    nc.vector.tensor_tensor(out, o[r, :, :, j, 0:HD], rec[r, :, :, j].unsqueeze(3).broadcast_to([64, 2, H // 2, HD]),
                                            ALU.mult).then_inc(out_read, 1)

            def add_out(f, fu, c):
                if cross and c == 7 and live(f - 2, UNITS):
                    wait(dve, o_ready, f - 1)
                    wait(dve, x1_biased, f - 1)
                    row = x_of(m, f - 2)
                    nc.vector.tensor_tensor(row, bank(7)[:, :].rearrange("p (q n) -> p q n", q=UT), row, ALU.add).then_inc(o_added, 1)

            pair = [None]

            def unit(su, u):
                f, fu = su + 1, 1 - u
                for c in range(UB):
                    n = UB * su + c
                    front(f, fu, c)
                    late(f, c)
                    shift(n, c)
                    if (c - 4) % 2 == 1:
                        normalize(n - 4, (c - 4) % 8, su if c >= 4 else su - 1, u if c >= 4 else fu)
                    add_out(f, fu, c)

            unit(-1, 1)
            unit(0, 0)
            unit(1, 1)
            with dve.Fori(1, UNITS // 2 - 1) as k:
                pair[0] = k
                unit(2 * k, 0)
                pair[0] = k + 1
                unit(2 * k + 1, 1)
            unit(UNITS - 2, 0)
            unit(UNITS - 1, 1)
            unit(UNITS, 0)
            unit(UNITS + 1, 1)


def routing(nc, a, m):
    with ExitStack() as stack:
        s = Memory(nc)
        stack.enter_context(s.ctx)
        tables = s.sem("tables")
        exp_ready, counts_ready, counted, step = (s.sem(n) for n in ("exp_ready", "counts_ready", "counted", "step"))
        shifted_logits, probs_moved, thr_kept, thr_back, hot_ready, counted_hot = (
            s.sem(n) for n in ("shifted_logits", "probs_moved", "thr_kept", "thr_back", "hot_ready", "counted_hot"))
        probs_done, thr_done, rows_done, slots_done, scattered = (
            s.sem(n) for n in ("probs_done", "thr_done", "rows_done", "slots_done", "scattered"))
        ps_c = s.ps("ps_c", [P, 2, E * UNITS])
        ps_n = s.ps("ps_n", [P, 512])
        ps_w = s.ps("ps_w", [P, E, TILES])
        ps_s = s.ps("ps_s", [P, E, TILES])
        lg = m.lg
        prx = s.sb("prx", [P, CAP // 2])
        hitx = s.sb("hitx", [P, CAP // 2])
        thrx, candx, cntx = (s.sb(n, [P, 1]) for n in ("thrx", "candx", "cntx"))
        flagx = s.sb("flagx", [P, 1], I32)
        same = s.sb("same", [P, P])
        within = s.sb("within", [P, E, TILES])
        hot = s.sb("hot", [P, E, TILES])
        hotb = s.sb("hotb", [P, E, TILES], BF16)
        carry = s.sb("carry", [P, E, TILES])
        upto = s.sb("upto", [P, E, TILES])
        used = s.sb("used", [P, E])
        usedi = s.sb("usedi", [P, E], I32)
        ends = s.sb("ends", [P, E])
        starts = s.sb("starts", [P, E])
        ones8 = s.sb("ones8", [P, E])
        slots = s.sb("slots", [P, TILES], I32)
        tau = s.sb("tau", [P, NT])
        index = s.sb("index", [P, TILES], I32)
        past = s.sb("past", [P, NT, E])
        tile_e = s.sb("tile_e", [P, NT])
        pr = s.sb("pr", [P, E, TILES])
        red = s.sb("red", [P, TILES])
        thr = s.sb("thr", [P, E])
        cand = s.sb("cand", [P, E])
        hit = s.sb("hit", [P, E, TILES])
        cnt = s.sb("cnt", [P, E])
        above = s.sb("above", [P, E, TILES])
        tie = s.sb("tie", [P, E, TILES])
        tierow = s.sb("tierow", [P, E, UNITS], BF16)
        rank = s.sb("rank", [P, E, TILES])
        base = s.sb("base", [P, E, UNITS])
        want = s.sb("want", [P, E])
        maski = s.sb("r_maski", [P, E, TILES], I32)
        key = s.sb("key", [P, E, TILES])
        best = s.sb("best", [P, TILES])
        free = s.sb("free", [P, TILES], I32)
        taken = s.sb("taken", [P, TILES])
        block = stack.enter_context(nc.Block())

        @block.sync
        def _(sp):
            sp.dma_start(same[:, :], a["same_expert"]).then_inc(tables, 16)
            sp.dma_start(tau[:, :], a["tile_numbers"].partition_broadcast(P)).then_inc(tables, 16)
            sp.dma_start(index[:, :], a["token_index"]).then_inc(tables, 16)
            sp.wait_ge(probs_done, 1)
            for e in range(E):
                sp.dma_start(prx[16 * e:16 * e + 16, :], pr[:, e, :]).then_inc(probs_moved, 16)
            sp.wait_ge(thr_done, 1)
            sp.dma_start(m.thr_dram.rearrange("(e o) -> e o", o=1), thrx[0:P:16, :]).then_inc(thr_kept, 16)
            sp.wait_ge(thr_kept, 16)
            sp.dma_start(thr[:, :], m.thr_dram.partition_broadcast(P)).then_inc(thr_back, 16)
            sp.wait_ge(thr_back, 16)
            sp.wait_ge(tables, 48)

        @block.gpsimd
        def _(pool):
            pool.wait_ge(slots_done, 1)
            pool.wait_ge(rows_done, 2)

            for t in range(TILES):
                nc.gpsimd.indirect_dma_start(m.sorted, bass.IndirectOffsetOnAxis(ap=slots[:, t:t + 1], axis=0),
                                             m.rows[:, t // UT, t % UT, :], None).then_inc(scattered, 16)
            pool.wait_ge(scattered, 16 * TILES)

        @block.tensor
        def _(pe):
            pe.wait_ge(tables, 16)
            def count(i):
                pe.wait_ge(counts_ready, i + 1)
                nc.tensor.matmul(ps_c[:, 0, 0:1], same[:, :], cntx[:, :], start=True, stop=True).then_inc(counted, 1)
            count(0)
            with pe.Fori(1, BITS) as i:
                count(i)
            pe.wait_ge(counts_ready, BITS + 1)
            nc.tensor.matmul(ps_c[:, 0, 0:E], m.ones[:, :], cnt[:, :], start=True, stop=True).then_inc(counted, 1)
            pe.wait_ge(counts_ready, BITS + 2)
            rows = tierow[:, :, :].rearrange("p e h -> p (e h)")
            nc.tensor.matmul(ps_c[:, 0, :], m.beforeb[:, :], rows, start=True, stop=True)
            nc.tensor.matmul(ps_c[:, 1, :], m.onesb[:, :], rows, start=True, stop=True).then_inc(counted, 1)
            pe.wait_ge(hot_ready, 1)
            nc.tensor.matmul(ps_w[:, :, :], m.beforeb[:, :], hotb[:, :, :], start=True, stop=True).then_inc(counted_hot, 1)
            nc.tensor.matmul(ps_s[:, :, :], m.onesb[:, :], hotb[:, :, :], start=True, stop=True).then_inc(counted_hot, 1)

        @block.scalar
        def _(act):
            act.wait_ge(shifted_logits, 1)
            nc.scalar.activation(lg[:, :, :], lg[:, :, :], ACT.Exp).then_inc(exp_ready, 1)

        @block.vector
        def _(dve):
            done = [0]

            def then(ins):
                done[0] += 1
                ins.then_inc(step, 1)
                dve.wait_ge(step, done[0])

            wide = lambda t: t.unsqueeze(2).broadcast_to([P, TILES, E])
            per_expert = lambda t: t[:, :].unsqueeze(2).broadcast_to([P, E, TILES])
            per_token = lambda t: t[:, :].unsqueeze(1).broadcast_to([P, E, TILES])
            dve.wait_ge(tables, 48)
            nc.vector.tensor_copy(m.rows[:, :, :, INDEX].rearrange("p u q -> p (u q)").bitcast(I32), index[:, :]).then_inc(rows_done, 1)
            then(nc.vector.tensor_reduce(red[:, :], lg[:, :, :], AX.X, ALU.max))
            nc.vector.tensor_tensor(lg[:, :, :], lg[:, :, :], wide(red[:, :]), ALU.subtract).then_inc(shifted_logits, 1)
            dve.wait_ge(exp_ready, 1)
            then(nc.vector.tensor_reduce(red[:, :], lg[:, :, :], AX.X, ALU.add))
            then(nc.vector.reciprocal(red[:, :], red[:, :]))
            nc.vector.tensor_tensor(pr[:, :, :].rearrange("p e t -> p t e"), lg[:, :, :], wide(red[:, :]), ALU.mult).then_inc(probs_done, 1)
            then(nc.vector.memset(thrx[:, :], 0.0))
            dve.wait_ge(probs_moved, 16 * E)
            for i in range(BITS):
                then(nc.vector.tensor_scalar(candx[:, :].bitcast(I32), thrx[:, :].bitcast(I32), 1 << (BITS - 1 - i), None, ALU.bitwise_or))
                nc.vector.tensor_scalar(hitx[:, :], prx[:, :], candx[:, :], None, ALU.is_ge, ALU.add, accum_out=cntx[:, :])\
                    .then_inc(counts_ready, 1)
                dve.wait_ge(counted, i + 1)
                then(nc.vector.tensor_scalar(flagx[:, :], ps_c[:, 0, 0:1], float(CAP), None, ALU.is_ge))
                ins = nc.vector.copy_predicated(thrx[:, :], flagx[:, :], candx[:, :])
                if i < BITS - 1:
                    then(ins)
            ins.then_inc(thr_done, 1)
            dve.wait_ge(thr_back, 16)
            then(nc.vector.tensor_tensor(above[:, :, :], pr[:, :, :], per_expert(thr), ALU.is_gt))
            nc.vector.tensor_reduce(cnt[:, :], above[:, :, :], AX.X, ALU.add).then_inc(counts_ready, 1)
            dve.wait_ge(counted, BITS + 1)
            then(nc.vector.tensor_scalar(want[:, :], ps_c[:, 0, 0:E], -1.0, float(CAP), ALU.mult, ALU.add))
            then(nc.vector.tensor_tensor(tie[:, :, :], pr[:, :, :], per_expert(thr), ALU.is_equal))
            by_unit = lambda t: t[:, :, :].rearrange("p e (h q) -> p e h q", q=UT)
            then(nc.vector.tensor_reduce(base[:, :, :], by_unit(tie), AX.X, ALU.add))
            nc.vector.tensor_copy(tierow[:, :, :], base[:, :, :]).then_inc(counts_ready, 1)
            dve.wait_ge(counted, BITS + 2)
            in_unit = ps_c[:, 0, :].rearrange("p (e h) -> p e h", e=E)
            of_unit = ps_c[:, 1, :].rearrange("p (e h) -> p e h", e=E)
            then(nc.vector.memset(base[:, :, 0:1], 0.0))
            for h in range(1, UNITS):
                then(nc.vector.tensor_tensor(base[:, :, h], of_unit[:, :, h - 1], base[:, :, h - 1], ALU.add))
            then(nc.vector.tensor_tensor(base[:, :, :], in_unit, base[:, :, :], ALU.add))
            then(nc.vector.tensor_tensor(by_unit(rank)[:, :, :, 0], base[:, :, :], by_unit(tie)[:, :, :, 0], ALU.add))
            for q in range(1, UT):
                then(nc.vector.tensor_tensor(by_unit(rank)[:, :, :, q], by_unit(rank)[:, :, :, q - 1], by_unit(tie)[:, :, :, q], ALU.add))
            then(nc.vector.tensor_tensor(rank[:, :, :], rank[:, :, :], per_expert(want), ALU.is_le))
            then(nc.vector.tensor_tensor(tie[:, :, :], tie[:, :, :], rank[:, :, :], ALU.mult))
            then(nc.vector.tensor_tensor(maski[:, :, :], above[:, :, :], tie[:, :, :], ALU.add))
            then(nc.vector.memset(key[:, :, :], -1.0))
            then(nc.vector.copy_predicated(key[:, :, :], maski[:, :, :], pr[:, :, :]))
            then(nc.vector.tensor_reduce(best[:, :], key[:, :, :].rearrange("p e t -> p t e"), AX.X, ALU.max))
            then(nc.vector.tensor_scalar(free[:, :], best[:, :], 0.0, None, ALU.is_lt))
            for e in range(E):
                then(nc.vector.copy_predicated(key[:, e, :], free[:, :], pr[:, e, :]))
            then(nc.vector.tensor_reduce(best[:, :], key[:, :, :].rearrange("p e t -> p t e"), AX.X, ALU.max))
            then(nc.vector.tensor_tensor(hit[:, :, :], key[:, :, :], per_token(best), ALU.is_equal))
            then(nc.vector.memset(taken[:, :], 0.0))
            for e in range(E):
                then(nc.vector.tensor_tensor(hot[:, e, :], hit[:, e, :], taken[:, :], ALU.is_gt))
                then(nc.vector.tensor_tensor(taken[:, :], taken[:, :], hit[:, e, :], ALU.max))
            nc.vector.tensor_copy(hotb[:, :, :], hot[:, :, :]).then_inc(hot_ready, 1)
            nc.vector.tensor_copy(m.rows[:, :, :, WEIGHT].rearrange("p u q -> p (u q)"), best[:, :]).then_inc(rows_done, 1)
            then(nc.vector.memset(carry[:, :, :], 1.0))
            then(nc.vector.memset(carry[:, :, 0:1], 0.0))
            then(nc.vector.memset(ones8[:, :], 1.0))
            dve.wait_ge(counted_hot, 2)
            flat = lambda t: t[:, :, :].rearrange("p e t -> p (e t)")
            then(nc.vector.tensor_tensor_scan(flat(upto), flat(carry), flat(ps_s), 0.0, ALU.mult, ALU.add))
            then(nc.vector.tensor_tensor(within[:, :, :], upto[:, :, :], ps_s[:, :, :], ALU.subtract))
            then(nc.vector.tensor_tensor(within[:, :, :], within[:, :, :], ps_w[:, :, :], ALU.add))
            then(nc.vector.tensor_scalar(usedi[:, :], upto[:, :, TILES - 1], float(P - 1), None, ALU.add))
            then(nc.vector.tensor_scalar(usedi[:, :], usedi[:, :], 7, None, ALU.arith_shift_right))
            then(nc.vector.tensor_copy(used[:, :], usedi[:, :]))
            then(nc.vector.tensor_tensor_scan(ends[:, :], ones8[:, :], used[:, :], 0.0, ALU.mult, ALU.add))
            then(nc.vector.tensor_tensor(starts[:, :], ends[:, :], used[:, :], ALU.subtract))
            then(nc.vector.tensor_scalar(starts[:, :], starts[:, :], float(P), None, ALU.mult))
            then(nc.vector.tensor_tensor(within[:, :, :], within[:, :, :], per_expert(starts), ALU.add))
            then(nc.vector.tensor_tensor(within[:, :, :], within[:, :, :], hot[:, :, :], ALU.mult))
            then(nc.vector.tensor_reduce(red[:, :], within[:, :, :].rearrange("p e t -> p t e"), AX.X, ALU.add))
            nc.vector.tensor_copy(slots[:, :], red[:, :]).then_inc(slots_done, 1)
            then(nc.vector.tensor_tensor(past[:, :, :], tau[:, :].unsqueeze(2).broadcast_to([P, NT, E]),
                                         ends[:, :].unsqueeze(1).broadcast_to([P, NT, E]), ALU.is_ge))
            then(nc.vector.tensor_reduce(tile_e[:, :], past[:, :, :], AX.X, ALU.add))
            then(nc.vector.tensor_scalar(m.tile_expert[:, :], tile_e[:, :], float(E - 1), None, ALU.min))


def experts(nc, a, m, out):
    with ExitStack() as stack:
        s = Memory(nc)
        stack.enter_context(s.ctx)
        w_loaded, xn_ready, xt_ready, xt_copied = (s.sem("e_" + n) for n in ("w_loaded", "xn_ready", "xt_ready", "xt_copied"))
        h_ready, gelu_ready, turned, ht_copied = (s.sem("e_" + n) for n in ("h_ready", "gelu_ready", "turned", "ht_copied"))
        y_ready, o_ready = s.sem("e_y_ready"), s.sem("e_o_ready")
        row_loaded = [s.sem(f"row_loaded{i}") for i in range(RING)]
        scattered = [s.sem(f"out_scattered{i}") for i in range(RING)]
        px = [s.ps(f"px{i}", [P, P]) for i in range(2)]
        ph = [s.ps(f"ph{i}", [P, FF]) for i in range(2)]
        pg = [s.ps(f"pg{i}", [P, 2, P]) for i in range(2)]
        py = [s.ps(f"py{i}", [P, D]) for i in range(2)]
        w1 = s.sb("w1", [P, E, FF])
        w2 = s.sb("w2", [P, E, 2, D])
        row = s.sb("row", [P, RING, ROW])
        xn = s.sb("e_xn", [P, 2, D])
        xt = s.sb("e_xt", [P, 2, P])
        hs = s.sb("hs", [P, 2, FF])
        ht = s.sb("ht", [P, 2, 2, P])
        orow = s.sb("orow", [P, RING, D])
        block = stack.enter_context(nc.Block())

        def steps(eng, step, lag):
            for c in range(RING):
                step(c, c, 0)
            with eng.Fori(1, NT // RING) as k:
                for c in range(RING):
                    step(RING * k + c, c, k)
            for c in range(lag):
                step(NT + c, c, NT // RING)

        @block.sync
        def _(sp):
            sp.dma_start(w1[:, :, :], a["w1"]).then_inc(w_loaded, 16)
            sp.dma_start(w2[:, :, :, :], a["w2"]).then_inc(w_loaded, 16)

            def load(n, c, k):
                wait(sp, scattered[c], 16 * k)
                sp.dma_start(row[:, c, :], m.sorted[bass.ds(P * n, P), :]).then_inc(row_loaded[c], 16)
            steps(sp, load, 0)

        @block.tensor
        def _(pe):
            pe.wait_ge(w_loaded, 32)

            def step(n, c, k):
                if live(n, NT):
                    wait(pe, xn_ready, n + 1)
                    wait(pe, xt_copied, n - 1)
                    nc.tensor.transpose(px[c % 2][:, :], xn[:, c % 2, :], m.ident[:, :]).then_inc(xt_ready, 1)
                i = n - 1
                if live(i, NT):
                    e = pe.value_load(m.tile_expert[0:1, bass.ds(i, 1)], min_val=0, max_val=E - 1)
                    wait(pe, xt_copied, i + 1)
                    wait(pe, gelu_ready, i - 1)
                    nc.tensor.matmul(ph[(c - 1) % 2][:, :], xt[:, (c - 1) % 2, :], w1[:, bass.ds(e, 1), :].rearrange("p o n -> p (o n)"),
                                     start=True, stop=True).then_inc(h_ready, 1)
                i = n - 2
                if live(i, NT):
                    wait(pe, gelu_ready, i + 1)
                    wait(pe, ht_copied, i - 1)
                    for f in range(2):
                        last = nc.tensor.transpose(pg[c % 2][:, f, :], hs[:, c % 2, P * f:P * f + P], m.ident[:, :])
                    last.then_inc(turned, 1)
                i = n - 3
                if live(i, NT):
                    e = pe.value_load(m.tile_expert[0:1, bass.ds(i, 1)], min_val=0, max_val=E - 1)
                    wait(pe, ht_copied, i + 1)
                    wait(pe, o_ready, i - 1)
                    for f in range(2):
                        last = nc.tensor.matmul(py[(c - 3) % 2][:, :], ht[:, (c - 3) % 2, f, :],
                                                w2[:, bass.ds(e, 1), f, :].rearrange("p o n -> p (o n)"), start=(f == 0), stop=(f == 1))
                    last.then_inc(y_ready, 1)
            steps(pe, step, 3)

        @block.scalar
        def _(act):
            def step(n, c, k):
                if live(n, NT):
                    wait(act, xt_ready, n + 1)
                    wait(act, h_ready, n - 1)
                    nc.scalar.activation(xt[:, c % 2, :], px[c % 2][:, :], ACT.Copy).then_inc(xt_copied, 1)
                i = n - 1
                if live(i, NT):
                    wait(act, h_ready, i + 1)
                    wait(act, turned, i - 1)
                    nc.scalar.activation(hs[:, (c - 1) % 2, :], ph[(c - 1) % 2][:, :], ACT.Gelu).then_inc(gelu_ready, 1)
            steps(act, step, 1)

        @block.vector
        def _(dve):
            def step(n, c, k):
                if live(n, NT):
                    dve.wait_ge(row_loaded[c], 16 * (k + 1))
                    wait(dve, xt_ready, n - 1)
                    nc.vector.tensor_scalar(xn[:, c % 2, :], row[:, c, 0:D], row[:, c, MEAN:MEAN + 1], row[:, c, RSTD:RSTD + 1],
                                            ALU.subtract, ALU.mult).then_inc(xn_ready, 1)
                i = n - 2
                if live(i, NT):
                    wait(dve, turned, i + 1)
                    wait(dve, y_ready, i - 1)
                    nc.vector.tensor_copy(ht[:, c % 2, :, :], pg[c % 2][:, :, :]).then_inc(ht_copied, 1)
                i, at = n - 3, (c - 3) % RING
                if live(i, NT):
                    wait(dve, y_ready, i + 1)
                    wait(dve, scattered[at], 16 * (k if c >= 3 else k - 1))
                    nc.vector.scalar_tensor_tensor(out=orow[:, at, :], in0=py[(c - 3) % 2][:, :], scalar=row[:, at, WEIGHT:WEIGHT + 1],
                                                   in1=row[:, at, 0:D], op0=ALU.mult, op1=ALU.add).then_inc(o_ready, 1)
            steps(dve, step, 3)

        @block.gpsimd
        def _(pool):
            def scatter(n, c, k):
                wait_apart(pool, o_ready, n + 1)
                nc.gpsimd.indirect_dma_start(out, bass.IndirectOffsetOnAxis(ap=row[:, c, INDEX:ROW].bitcast(I32), axis=0),
                                             orow[:, c, :], None, bounds_check=B * T - 1, oob_is_err=False).then_inc(scattered[c], 16)
            steps(pool, scatter, 0)
            for c in range(RING):
                pool.wait_ge(scattered[c], 16 * (NT // RING))


def decoder_layer(nc, a, out):
    m = Memory(nc)
    sorted_rows = nc.dram_tensor("sorted_rows", (NT * P, ROW), F32, kind="Internal").ap()
    with m.ctx:
        m.ident = m.sb("ident", [P, P])
        m.qscale = m.sb("qscale", [P, C])
        m.dupf = m.sb("dupf", [P, P])
        m.dup = m.sb("dup", [P, P], BF16)
        m.before = m.sb("before", [P, P])
        m.beforeb = m.sb("beforeb", [P, P], BF16)
        m.ones = m.sb("ones", [P, P])
        m.onesb = m.sb("onesb", [P, P], BF16)
        m.wg = m.sb("wg", [P, E])
        m.tb = m.sb("tb", [P, T])
        m.gates = m.sb("gates", [P, 4])
        m.maski = m.sb("maski", [P, T], I32)
        m.maskf = m.sb("maskf", [P, T])
        m.maskb = m.sb("maskb", [P, T], BF16)
        m.tb_hi, m.tb_mid, m.tb_lo, m.tb_hm = (m.sb(n, [P, T], BF16) for n in ("tb_hi", "tb_mid", "tb_lo", "tb_hm"))
        m.tb_rest = m.sb("tb_rest", [P, T])
        m.bo_row = m.sb("bo_row", [P, 2, D])
        m.wo = m.sb("wo", [P, 2, D])
        m.wqkv = m.sb("wqkv", [P, 2, 3, D])
        m.bqk = m.sb("bqk", [P, 2, 2])
        m.bv = m.sb("bv", [P, 2, UB * T])
        m.rows = m.sb("rows", [P, UNITS, UT, ROW])
        m.x = m.rows[:, :, :, 0:D]
        m.lg = m.sb("lg", [P, TILES, E])
        m.pad = m.sb("pad", [P, ROW])
        m.tile_expert = m.sb("tile_expert", [P, NT], I32)
        m.thr_dram = nc.dram_tensor("thresholds", (E,), F32, kind="Internal").ap()
        m.sorted = sorted_rows
        m.ctx_ = m.sb("ctx", [P, H // 2, HD, B])
        att = ExitStack()
        keep, m.ctx = m.ctx, att
        m.ctxt = m.sb("ctxt", [P, H, UT, B])
        m.qexp = m.sb("qexp", [P, 2, UB, C, T])
        m.kexp = m.sb("kexp", [P, 2, UB, G, T])
        m.vb = m.sb("vb", [P, 2, UB * 4, 2, 2, OW])
        m.ctx = m.ctx_
        setup(nc, a, m)
        attention(nc, a, m, False)
        attention(nc, a, m, True)
        att.close()
        routing(nc, a, m)
        experts(nc, a, m, out)
        m.ctx = keep


def kernel(**inputs):
    import numpy as np
    import concourse.bacc as bacc
    from concourse.bass_utils import run_bass_kernel_spmd

    w = {k: np.asarray(v) for k, v in inputs.items()}
    at, xa = "L0_attn_", "L0_xattn_"
    pos = np.arange(T)
    rows = np.stack([w[at + "time_bias"][0, 0, 250 - q:250 - q + T] for q in range(T)])
    mask = w["mask_1x1xSxS2_ik0"][0, 0]
    dup = (pos[:, None] == pos[None, :]).astype(np.float32)
    token_index = (P * UT * np.arange(UNITS)[None, :, None] + UT * np.arange(P)[:, None, None] + np.arange(UT)[None, None, :])
    token_index = token_index.reshape(P, TILES).astype(np.int32)
    arrays = {
        "x_tiles": w["x"].reshape(UNITS, UT, P, D),
        "x_rows": w["x"].reshape(UNITS, P, UT * D),
        "ctx_tiles": w["ctx_1024"].reshape(UNITS, UT, P, D),
        "ident": np.eye(P, dtype=np.float32),
        "class_scale": ((np.arange(P)[:, None] % 32) // HD == np.arange(C)[None, :]).astype(np.float32) * np.float32(HD ** -0.5),
        "dup": np.tile(dup, (2, 2)),
        "before": (np.arange(P)[:, None] < np.arange(P)[None, :]).astype(np.float32),
        "wg": w["L0_ffn_Wg"],
        "same_expert": (np.arange(P)[:, None] // 16 == np.arange(P)[None, :] // 16).astype(np.float32),
        "tile_numbers": np.arange(NT, dtype=np.float32),
        "token_index": token_index,
        "time_tile": np.concatenate([rows, rows]),
        "et_gate": w[at + "et_gate"].reshape(1),
        "is_gate": w[at + "is_gate"].reshape(1),
        "mask_tile": np.concatenate([mask, mask]),
        "self_bo": w[at + "bo"],
        "cross_bo": w[xa + "bo"],
        "cross_wo": w[xa + "wo"].T.reshape(H // 2, 2, HD, D).transpose(1, 0, 2, 3).reshape(P, D),
        "self_wo": w[at + "Wo"].T,
        "w1": w["L0_ffn_W1"].transpose(1, 0, 2),
        "w2": w["L0_ffn_W2"].reshape(E, 2, P, D).transpose(2, 0, 1, 3),
    }
    for who, p, up in (("self", at, True), ("cross", xa, False)):
        for x in "qkv":
            arrays[f"{who}_w{x}"] = w[p + ("W" if up else "w") + x].T
            b = w[p + "b" + x]
            arrays[f"{who}_b{x}"] = b.reshape(P, 1)
        arrays[f"{who}_bv"] = np.tile(b.reshape(G // 2, 2, C * HD).transpose(1, 0, 2).reshape(2, -1), (1, UB))
    arrays = {k: np.ascontiguousarray(v) for k, v in arrays.items()}
    nc = bacc.Bacc("TRN2", target_bir_lowering=False, num_devices=1)
    aps = {k: nc.dram_tensor(k + "_dram", v.shape, mybir.dt.from_np(v.dtype), kind="ExternalInput").ap() for k, v in arrays.items()}
    out = nc.dram_tensor("out_dram", (B * T, D), F32, kind="ExternalOutput").ap()
    decoder_layer(nc, aps, out)
    r = run_bass_kernel_spmd(nc, [{k + "_dram": v for k, v in arrays.items()}], core_ids=[0])
    return r.results[0]["out_dram"].reshape(B, T, D)
```

```python
from contextlib import ExitStack

import concourse.bass as bass
from concourse import mybir

F32 = mybir.dt.float32
BF16 = mybir.dt.bfloat16
F16 = mybir.dt.float16
I32 = mybir.dt.int32
ALU = mybir.AluOpType
ACT = mybir.ActivationFunctionType
AX = mybir.AxisListType

P = 128
B, T, D = 128, 64, 128
H, HD = 16, 8
C = P // 32
G = H // C
NPAIR = C // 2
UB = 8
UNITS = B // UB
UT = UB * T // P
SW = G * T
OW = HD + 1
OB = H * OW
E, FF = 8, 256
TILES = B * T // P
CAP = B * T // E
NT = TILES + E
ROW = D + 4
MEAN, RSTD, WEIGHT, INDEX = range(D, ROW)
BITS = 30
ROUNDS = BITS // 2
SHARE = CAP // 4
RING = 12
EPS = 1e-5
MASKED = -1e30


def known(v):
    return isinstance(v, int)


def wait(eng, sem, value):
    if not known(value) or value > 0:
        eng.wait_ge(sem, value)


def wait_apart(eng, sem, value):
    wait(eng, sem, value)
    if not known(value):
        eng.nop(nofuse=True)


def at_most(value, most):
    return min(value, most) if known(value) else value


def live(n, count):
    return not known(n) or 0 <= n < count


def units(eng, unit):
    unit(-1, 1)
    unit(0, 0)
    unit(1, 1)
    with eng.Fori(1, UNITS // 2 - 1) as k:
        unit(2 * k, 0)
        unit(2 * k + 1, 1)
    unit(UNITS - 2, 0)
    unit(UNITS - 1, 1)
    unit(UNITS, 0)
    unit(UNITS + 1, 1)


NEWTON = 3


def guess_rstd(nc, dve, var, veps, guess, moments_ready, guessed, i):
    dve.wait_ge(moments_ready, UT * (i + 1))
    nc.vector.tensor_scalar(veps, var, EPS, None, ALU.add).then_inc(guessed, 1)
    dve.wait_ge(guessed, 3 * i + 1)
    nc.vector.tensor_scalar(guess.bitcast(I32), veps.bitcast(I32), 1, None, ALU.arith_shift_right).then_inc(guessed, 1)
    dve.wait_ge(guessed, 3 * i + 2)
    nc.vector.tensor_scalar(guess.bitcast(I32), guess.bitcast(I32), -1.0, float(0x5F3759DF), ALU.mult, ALU.add).then_inc(guessed, 1)


def refine_rstd(nc, pool, veps, y, t, guessed, refined, i):
    wait_apart(pool, guessed, 3 * i + 3)
    for k in range(NEWTON):
        done = 4 * NEWTON * i + 4 * k
        if k:
            wait_apart(pool, refined, done)
        nc.gpsimd.tensor_tensor(t, y, y, ALU.mult).then_inc(refined, 1)
        wait_apart(pool, refined, done + 1)
        nc.gpsimd.tensor_tensor(t, t, veps, ALU.mult).then_inc(refined, 1)
        wait_apart(pool, refined, done + 2)
        nc.gpsimd.tensor_scalar(t, t, -0.5, 1.5, ALU.mult, ALU.add).then_inc(refined, 1)
        wait_apart(pool, refined, done + 3)
        nc.gpsimd.tensor_tensor(y, y, t, ALU.mult).then_inc(refined, 1)


def x_of(m, i):
    return m.x[:, bass.ds(i, 1), :, :].rearrange("p o q n -> p (o q) n")


class Memory:

    def __init__(self, nc):
        self.nc = nc
        self.ctx = ExitStack()

    def sb(self, name, shape, dt=F32):
        return self.ctx.enter_context(self.nc.sbuf_tensor(name, shape, dt))

    def ps(self, name, shape, dt=F32):
        return self.ctx.enter_context(self.nc.psum_tensor(name, shape, dt))

    def sem(self, name):
        return self.ctx.enter_context(self.nc.semaphore(name))


def other_rows(jj):
    return slice(64 * (1 - jj), 64 * (1 - jj) + 64)


def lay_table(nc, m, table, laid):
    for u in range(2):
        for jj in range(NPAIR):
            r = other_rows(jj)
            nc.vector.tensor_copy(m.kexp[r, u, :, jj, :, :], table[r, :].unsqueeze(1).unsqueeze(1).broadcast_to([64, UB, G, T]))\
                .then_inc(laid, 1)


def setup(nc, a, m):
    with ExitStack() as stack:
        s = Memory(nc)
        stack.enter_context(s.ctx)
        first_loaded, loaded, zeroed, padded = (s.sem(n) for n in ("first_loaded", "loaded", "zeroed", "padded"))
        gate, table, tmask, laid = (s.sem(n) for n in ("gate_ready", "table_ready", "mask_ready", "laid"))
        block = stack.enter_context(nc.Block())
        first_loads = [
            (m.gates[:, 0:2], a["gates"].partition_broadcast(P)),
            (m.tb[:, :], a["time_tile"]),
            (m.consts[:, :, :], a["consts"]),
        ]
        loads = [
            (m.gmask[:, :], a["group_mask"]),
            (m.bqk[:, :, :], a["bqk"]),
            (m.maski[:, :], a["mask_tile"]),
            (m.wqkv[:, :, :, :], a["wqkv"]),
            (m.bo_row[:, :, :], a["bo"].partition_broadcast(P)),
            (m.wo[:, :, :], a["wo"]),
            (m.wg[:, :], a["wg"]),
        ]
        loads += [(m.bv[64 * gh:64 * gh + 64, :, :], a["bv"][gh].partition_broadcast(64)) for gh in range(2)]

        @block.sync
        def _(sp):
            for out, in_ in first_loads:
                sp.dma_start(out, in_).then_inc(first_loaded, 16)
            for out, in_ in loads:
                sp.dma_start(out, in_).then_inc(loaded, 16)
            sp.wait_ge(first_loaded, 16 * len(first_loads))
            sp.wait_ge(loaded, 16 * len(loads))

        @block.gpsimd
        def _(pool):
            nc.gpsimd.memset(m.qexp[:, :, :, :, :], 0.0).then_inc(zeroed, 1)
            nc.gpsimd.memset(m.vb[:, :, :, :, :, :], 0.0).then_inc(zeroed, 1)
            pool.wait_ge(zeroed, 2)
            for gh in range(2):
                nc.gpsimd.memset(m.vb[64 * gh:64 * gh + 64, :, :, :, gh, HD:OW], 1.0).then_inc(zeroed, 1)
            pool.wait_ge(zeroed, 4)
            nc.gpsimd.memset(m.pad[:, 0:INDEX], 0.0).then_inc(padded, 1)
            nc.gpsimd.memset(m.pad[:, INDEX:ROW].bitcast(I32), B * T).then_inc(padded, 1)

        @block.scalar
        def _(act):
            act.wait_ge(first_loaded, 16 * len(first_loads))
            nc.scalar.activation(m.gates[:, 2:3], m.gates[:, 0:1], ACT.Sigmoid).then_inc(gate, 1)
            act.wait_ge(zeroed, 1)
            for u in range(2):
                for jj in range(NPAIR):
                    r = other_rows(jj)
                    nc.scalar.activation(m.qexp[r, u, :, 2 * jj:2 * jj + 2, :].rearrange("p b c q -> p b (c q)"),
                                         m.dup[r, :].unsqueeze(1).broadcast_to([64, UB, 2 * T]), ACT.Copy).then_inc(laid, 1)

        @block.vector
        def _(dve):
            dve.wait_ge(first_loaded, 16 * len(first_loads))
            nc.vector.memset(m.ones[:, :], 1.0)
            nc.vector.memset(m.onesb[:, :], 1.0)
            nc.vector.tensor_copy(m.beforeb[:, :], m.before[:, :])
            dve.wait_ge(gate, 1)
            nc.vector.tensor_scalar(m.tb[:, :], m.tb[:, :], m.gates[:, 2:3], m.gates[:, 1:2], ALU.mult, ALU.add).then_inc(table, 1)
            dve.wait_ge(table, 1)
            lay_table(nc, m, m.tb, laid)
            dve.wait_ge(loaded, 16 * len(loads))
            nc.vector.tensor_copy(m.maskf[:, :], m.maski[:, :]).then_inc(tmask, 1)
            dve.wait_ge(tmask, 1)
            nc.vector.tensor_scalar(m.maskf[:, :], m.maskf[:, :], 0.0, MASKED, ALU.is_equal, ALU.mult).then_inc(tmask, 1)
            for n in range(2):
                nc.vector.tensor_scalar(m.bkg[:, n, :], m.gmask[:, :], m.bqk[:, n, 1:2], None, ALU.mult).then_inc(tmask, 1)


def attention(nc, a, m, cross):
    n_att = 1 if cross else 0
    pre = "cross_" if cross else "self_"
    with ExitStack() as stack:
        s = Memory(nc)
        stack.enter_context(s.ctx)
        sem = lambda name: s.sem(pre + name)
        scores_ready, max_ready, shifted = sem("scores_ready"), sem("max_ready"), sem("shifted")
        probs_ready, turned, turned_copied = sem("probs_ready"), sem("turned"), sem("turned_copied")
        out_ready, recip_ready, out_read = sem("out_ready"), sem("recip_ready"), sem("out_read")
        x_loaded = [sem(f"x_loaded{u}") for u in range(2)]
        stats_ready, moments_ready, guessed, xn_ready = (sem(n) for n in ("stats_ready", "moments_ready", "guessed", "xn_ready"))
        refined = sem("refined")
        xt_ready, xt_copied = sem("xt_ready"), sem("xt_copied")
        k_copied, k_ready_by_pool = sem("k_copied"), sem("k_ready_by_pool")
        q_done, q_ready, k_done, k_ready, v_done, v_ready = (sem(n) for n in ("q_done", "q_ready", "k_done", "k_ready", "v_done", "v_ready"))
        if cross:
            c_loaded = [sem(f"c_loaded{u}") for u in range(2)]
            y_copied, y_ready, x_biased, x1_ready, x1_biased = (sem(n) for n in ("y_copied", "y_ready", "x_biased", "x1_ready", "x1_biased"))
            ct_ready, ct_copied, c2_turned, c2_copied, o_ready, o_added = (sem(n) for n in ("ct_ready", "ct_copied", "c2_turned", "c2_copied", "o_ready", "o_added"))

        sc = [s.ps(f"{pre}sc{i}", [P, NPAIR, G, T]) for i in range(2)]
        pt = [s.ps(f"{pre}pt{i}", [P, 4, P]) for i in range(2)]
        po = [s.ps(f"{pre}po{i}", [P, 512]) for i in range(2)]
        job = [s.ps(f"{pre}job{i}", [P, 512]) for i in range(2)]
        xin = s.sb(pre + "xin", [P, 2, UT, D])
        xn = s.sb(pre + "xn", [P, UT, D])
        xnt = s.sb(pre + "xnt", [P, UT * P])
        stats = s.sb(pre + "stats", [P, UT, 6])
        moments = s.sb(pre + "moments", [P, UT, 2])
        rstd, veps, newton = (s.sb(pre + n, [P, UT]) for n in ("rstd", "veps", "newton"))
        mx = s.sb(pre + "mx", [P, 2, NPAIR * G])
        sh = s.sb(pre + "sh", [P, 4, NPAIR * G * T])
        pts = s.sb(pre + "pts", [P, 2, 4, P])
        rec = s.sb(pre + "rec", [P, 2, H // 2, 2])
        if cross:
            cin = s.sb(pre + "cin", [P, 2, UT, D])
            ct = s.sb(pre + "ct", [P, UT * P])
            yctx = s.sb(pre + "yctx", [P, UT, B])
            ctx_moved = [sem(f"ctx_moved{j}") for j in range(2)]
            laid = sem("laid")
            ctx_moved_by_pool = sem("ctx_moved_by_pool")
            stats2 = s.sb(pre + "stats2", [P, UT, 6])
            moments2 = s.sb(pre + "moments2", [P, UT, 2])
            rstd2, veps2, newton2 = (s.sb(pre + n, [P, UT]) for n in ("rstd2", "veps2", "newton2"))
            xn2 = s.sb(pre + "xn2", [P, UT, D])
            xn2t = s.sb(pre + "xn2t", [P, UT * P])
            stats2_ready, moments2_ready, guessed2, refined2, xn2_ready = (
                sem(n) for n in ("stats2_ready", "moments2_ready", "guessed2", "refined2", "xn2_ready"))
            xn2_turned, xn2_copied, logits_ready, logits_read, kept = (
                sem(n) for n in ("xn2_turned", "xn2_copied", "logits_ready", "logits_read", "kept"))
            c2 = s.sb(pre + "c2", [P, 2, UB, H // 2, HD])
            c2t = s.sb(pre + "c2t", [P, UB // 2, 2, T])
        kvt = ct if cross else xnt
        if not cross:
            kt = s.sb(pre + "kt", [P, UT * P])
        wq, wk, wv = (m.wqkv[:, n_att, w, :] for w in range(3))
        block = stack.enter_context(nc.Block())

        def po_view(pair):
            return po[pair % 2][:, 0:2 * OB].rearrange("p (b h j w) -> p b h j w", b=2, h=H // 2, j=2)

        def turn_context(eng, j, q, moved):
            rows = 64 * j + 16 * q
            for d in range(HD):
                eng.dma_start(m.ctxt[d:P:HD, H // 2 * j:H // 2 * (j + 1), q, :], m.ctx[rows:rows + 16, :, d, :]).then_inc(moved, 16)

        def keys_of(fu):
            return xin[:, fu, :, :].rearrange("p q n -> p (q n)") if cross else kt[:, :]

        def bank(j):
            return job[j % 2]

        @block.sync
        def _(sp):

            def unit(su, u):
                f, fu = su + 1, 1 - u
                if not live(f, UNITS):
                    return
                if cross:
                    wait_apart(sp, x1_ready, f - 1)
                    wait_apart(sp, k_ready, G * (f - 1))
                    wait_apart(sp, k_ready_by_pool, G * (f - 1))
                    sp.dma_start(xin[:, fu, :, :], a["x_rows"][bass.ds(f, 1)].rearrange("o b n -> (o b) n")
                                 .rearrange("b (q n) -> b q n", q=UT)).then_inc(x_loaded[fu], 16)
                    wait(sp, ct_ready, f - 1)
                    sp.dma_start(cin[:, fu, :, :], a["ctx_tiles"][bass.ds(f, 1)].rearrange("o t p n -> (o p) t n"))\
                        .then_inc(c_loaded[fu], 16)
                    if known(f) and f < 2:
                        for q in range(UT if f else UT - 1):
                            turn_context(sp, f, q, ctx_moved[f])
                else:
                    wait(sp, xn_ready, UT * (f - 1))
                    sp.dma_start(xin[:, fu, :, :], a["x_tiles"][bass.ds(f, 1)].rearrange("o t p n -> (o p) t n"))\
                        .then_inc(x_loaded[fu], 16)
            units(sp, unit)
            if not cross:
                sp.dma_start(m.sorted.rearrange("(t p) n -> p t n", p=P), m.pad[:, :].unsqueeze(1).broadcast_to([P, NT, ROW]))\
                    .then_inc(m.filled, 16)

        @block.gpsimd
        def _(pool):
            def unit(su, u):
                f, fu = su + 1, 1 - u
                if not cross:
                    if live(f, UNITS):
                        refine_rstd(nc, pool, veps[:, :], rstd[:, :], newton[:, :], guessed, refined, f)
                        spread_k(f, fu)
                    return
                if live(f, UNITS):
                    if known(f) and f == 0:
                        turn_context(pool, 0, UT - 1, ctx_moved_by_pool)
                        pool.wait_ge(ctx_moved_by_pool, 16 * HD)
                        move_ctx(0)
                    pool.wait_ge(x_loaded[fu], 16 * (pair_of(f) + 1))
                    nc.gpsimd.tensor_tensor(xin[:, fu, :, :], xin[:, fu, :, :], bo_tiles(0), ALU.add).then_inc(x_biased, 1)
                z = f - 3
                if live(z, UNITS):
                    refine_rstd(nc, pool, veps2[:, :], rstd2[:, :], newton2[:, :], guessed2, refined2, z)
                    wait_apart(pool, refined2, 4 * NEWTON * (z + 1))
                    for src, col in ((moments2[:, :, 0], MEAN), (rstd2[:, :], RSTD)):
                        nc.gpsimd.tensor_copy(m.rows[:, bass.ds(z, 1), :, col].rearrange("p o q -> p (o q)"), src).then_inc(kept, 1)
                if live(f, UNITS):
                    refine_rstd(nc, pool, veps[:, :], rstd[:, :], newton[:, :], guessed, refined, f)
                    pool.wait_ge(xn_ready, UT * (f + 1))
                    nc.gpsimd.tensor_tensor(x_of(m, f), x_of(m, f), bo_tiles(1), ALU.add).then_inc(x1_biased, 1)
                    spread_k(f, fu)
                if live(f + 1, UNITS):
                    move_ctx(f + 1)

            def spread_k(f, fu):
                wait_apart(pool, k_copied, f + 1)
                wait_apart(pool, refined, 4 * NEWTON * (f + 1))
                if cross:
                    wait_apart(pool, x1_biased, f + 1)
                for g in range(G):
                    nc.gpsimd.tensor_scalar(m.kexp[64:128, fu, :, 1, g, :], keys_of(fu)[64:128, :].rearrange("p (b k) -> p b k", b=UB),
                                            m.gmask[64:128, g:g + 1], m.bkg[64:128, n_att, g:g + 1], ALU.mult, ALU.add)\
                        .then_inc(k_ready_by_pool, 1)
                wait_apart(pool, k_ready_by_pool, G * (f + 1))

            def move_ctx(f):
                if known(f) and f == 0:
                    pool.wait_ge(ctx_moved[0], 16 * HD * (UT - 1))
                if known(f) and f == 2:
                    pool.wait_ge(ctx_moved[1], 16 * HD * UT)
                wait(pool, y_ready, f)
                nc.gpsimd.tensor_copy(yctx[:, :, :], m.ctxt[:, bass.ds(f, 1), :, :].rearrange("p o q b -> p (o q) b"))\
                    .then_inc(y_copied, 1)

            def bo_tiles(n):
                return m.bo_row[:, n, :].unsqueeze(1).broadcast_to([P, UT, D])

            def pair_of(f):
                if known(f):
                    return f // 2
                return pairs[0]

            pairs = [None]

            unit(-1, 1)
            unit(0, 0)
            unit(1, 1)
            with pool.Fori(1, UNITS // 2 - 1) as k:
                pairs[0] = k
                unit(2 * k, 0)
                pairs[0] = k + 1
                unit(2 * k + 1, 1)
            unit(UNITS - 2, 0)
            unit(UNITS - 1, 1)
            unit(UNITS, 0)
            unit(UNITS + 1, 1)

        @block.tensor
        def _(pe):
            def scores(n, c, su, u):
                if not live(n, B):
                    return
                wait(pe, shifted, n - 1)
                if c == 0:
                    wait(pe, q_ready, su + 1)
                    wait(pe, k_ready, G * (su + 1))
                    wait(pe, k_ready_by_pool, G * (su + 1))
                    if cross and known(su) and su == 0:
                        pe.wait_ge(laid, 2 * NPAIR)
                for jj in range(NPAIR):
                    last = nc.tensor.matmul(sc[c % 2][:, jj, :, :], m.qexp[:, u, c, 2 * jj:2 * jj + 2, :], m.kexp[:, u, c, jj, :, :],
                                            start=True, stop=True)
                last.then_inc(scores_ready, 1)

            def turn(n, c):
                if not live(n, B):
                    return
                wait(pe, probs_ready, n + 1)
                wait(pe, turned_copied, n - 1)
                for i in range(4):
                    last = nc.tensor.transpose(pt[c % 2][:, i, :], sh[:, c % 4, P * i:P * i + P], m.ident[:, :])
                last.then_inc(turned, 1)

            def values(n, c, u, su):
                if not live(n, B):
                    return
                wait(pe, turned_copied, n + 1)
                if c == 0:
                    wait(pe, v_ready, 2 * (su + 1))
                if c % 2 == 0:
                    wait(pe, out_read, n - 2)
                o = po_view(c // 2)
                for jj in range(NPAIR):
                    for gp in range(G // 2):
                        out = o[:, c % 2, 4 * gp + jj:4 * gp + jj + 3:2, :, :].rearrange("p g j w -> p j g w")
                        last = nc.tensor.matmul(out, pts[:, c % 2, 2 * jj + gp, :], m.vb[:, u, 4 * c + 2 * gp + jj, :, :, :],
                                                start=True, stop=True)
                last.then_inc(out_ready, 1)

            def turn_tiles(out, tiles, sem_):
                for t in range(UT):
                    last = nc.tensor.transpose(out[:, P * t:P * t + P], tiles[:, t, :], m.ident[:, :])
                last.then_inc(sem_, 1)

            def turn_x(f, fu, j):
                pe.wait_ge(xn_ready, UT * (f + 1))
                turn_tiles(bank(j), xn, xt_ready)

            def project_q(f, fu, j):
                pe.wait_ge(xt_copied, f + 1)
                nc.tensor.matmul(bank(j)[:, :], wq, xnt[:, :], start=True, stop=True).then_inc(q_done, 1)

            def project_k(f, fu, j):
                pe.wait_ge(ct_copied if cross else xt_copied, f + 1)
                nc.tensor.matmul(bank(j)[:, :], wk, kvt[:, :], start=True, stop=True).then_inc(k_done, 1)

            def project_v(f, fu, j):
                for gh in range(2):
                    w = wv.rearrange("p (gp g c) -> p gp g c", g=2, c=C * HD)[:, :, gh, :]
                    for b in range(UB):
                        last = nc.tensor.matmul(bank(j)[64 * gh:64 * gh + 64, T * b:T * b + T].rearrange("p (g c) -> p g c", g=G // 2),
                                                kvt[:, T * b:T * b + T], w, start=True, stop=True)
                last.then_inc(v_done, 1)

            def self_front(f, fu, c):
                if not live(f, UNITS):
                    return
                if c == 3:
                    wait(pe, q_ready, f)
                    turn_x(f, fu, 0)
                if c == 4:
                    wait(pe, v_ready, 2 * f)
                    project_k(f, fu, 1)
                if c == 5:
                    project_q(f, fu, 2)
                if c == 6:
                    wait(pe, k_copied, f + 1)
                    project_v(f, fu, 3)

            def cross_front(f, fu, c):
                if live(f, UNITS):
                    if c == 0:
                        wait(pe, xt_copied, f)
                        wait(pe, c2_copied, 4 * (f - 2))
                        pe.wait_ge(y_copied, f + 1)
                        for q in range(UT):
                            last = nc.tensor.matmul(bank(0)[:, D * q:D * q + D], yctx[:, q, :], m.wo[:, 0, :], start=True, stop=True)
                        last.then_inc(y_ready, 1)
                    if c == 1:
                        wait(pe, q_ready, f)
                        wait(pe, o_added, f - 2)
                        pe.wait_ge(c_loaded[fu], 16 * ((f // 2 if known(f) else pair[0]) + 1))
                        turn_tiles(bank(1), cin[:, fu, :, :], ct_ready)
                    if c == 2:
                        pe.wait_ge(x1_ready, f + 1)
                        project_k(f, fu, 2)
                    if c == 3:
                        project_v(f, fu, 3)
                    if c == 4:
                        wait(pe, k_copied, f + 1)
                        turn_x(f, fu, 4)
                    if c == 5:
                        wait(pe, v_ready, 2 * (f + 1))
                        project_q(f, fu, 5)
                z = f - 3
                if live(z, UNITS):
                    if c == 5:
                        wait(pe, xt_copied, at_most(f + 1, UNITS))
                        wait(pe, c2_copied, at_most(4 * (f - 2), 4 * UNITS))
                        wait(pe, xn2_ready, UT * (z + 1))
                        turn_tiles(bank(6), xn2, xn2_turned)
                if live(f - 2, UNITS):
                    if c == 6:
                        wait(pe, xn2_copied, z + 1)
                        wait(pe, xt_copied, at_most(f + 1, UNITS))
                        wait(pe, out_read, 8 * (f - 1))
                        wait(pe, c2_copied, 4 * (f - 2))
                        for t in range(UB // 2):
                            last = nc.tensor.transpose(bank(6)[:, P * t:P * t + P],
                                                       c2[:, fu, 2 * t:2 * t + 2, :, :].rearrange("p b h d -> p (b h d)"), m.ident[:, :])
                        last.then_inc(c2_turned, 1)
                if live(z, UNITS):
                    if c == 6:
                        wait(pe, q_ready, at_most(f + 1, UNITS))
                        wait(pe, o_added, at_most(f - 2, UNITS))
                        wait(pe, xn2_copied, z + 1)
                        for t in range(UT):
                            last = nc.tensor.matmul(bank(7)[:, E * t:E * t + E], xn2t[:, P * t:P * t + P], m.wg[:, :], start=True, stop=True)
                        last.then_inc(logits_ready, 1)
                if live(f - 2, UNITS):
                    if c == 7:
                        wait(pe, logits_read, z + 1)
                        wait(pe, q_ready, at_most(f + 1, UNITS))
                        wait(pe, o_added, f - 2)
                        wait(pe, c2_copied, 4 * (f - 1))
                        tok = c2t[:, :, :, :].rearrange("p b c (t q) -> p q (b c t)", q=UT)
                        for q in range(UT):
                            last = nc.tensor.matmul(bank(7)[:, D * q:D * q + D], tok[:, q, :], m.wo[:, 1, :],
                                                    start=True, stop=True)
                        last.then_inc(o_ready, 1)

            pair = [None]

            def unit(su, u):
                f, fu = su + 1, 1 - u
                for c in range(UB):
                    n = UB * su + c
                    scores(n, c, su, u)
                    turn(n - 2, (c - 2) % 8)
                    c3 = (c - 3) % 8
                    values(n - 3, c3, u if c >= 3 else fu, su if c >= 3 else su - 1)
                    (cross_front if cross else self_front)(f, fu, c)

            unit(-1, 1)
            unit(0, 0)
            unit(1, 1)
            with pe.Fori(1, UNITS // 2 - 1) as k:
                pair[0] = k
                unit(2 * k, 0)
                pair[0] = k + 1
                unit(2 * k + 1, 1)
            unit(UNITS - 2, 0)
            unit(UNITS - 1, 1)
            unit(UNITS, 0)
            unit(UNITS + 1, 1)

        @block.scalar
        def _(act):
            def unit(su, u):
                f, fu = su + 1, 1 - u
                for c in range(UB):
                    n = UB * su + c
                    if live(f, UNITS):
                        if cross and c == 2:
                            act.wait_ge(ct_ready, f + 1)
                            nc.scalar.activation(ct[:, :], bank(1)[:, :], ACT.Copy).then_inc(ct_copied, 1)
                        if c == (5 if cross else 4):
                            act.wait_ge(xt_ready, f + 1)
                            if cross:
                                nc.scalar.activation(xnt[:, :].rearrange("p (b q) -> p q b", q=UT),
                                                     bank(4)[:, :].rearrange("p (q b) -> p q b", q=UT), ACT.Copy).then_inc(xt_copied, 1)
                            else:
                                nc.scalar.activation(xnt[:, :], bank(0)[:, :], ACT.Copy).then_inc(xt_copied, 1)
                        if c == (3 if cross else 5):
                            act.wait_ge(k_done, f + 1)
                            wait(act, k_ready, G * f)
                            wait(act, k_ready_by_pool, G * f)
                            nc.scalar.activation(keys_of(fu), bank(2 if cross else 1)[:, :], ACT.Copy).then_inc(k_copied, 1)
                        for g in {0: (0,), 1: (1, 2), 2: (3,)}.get(c - (3 if cross else 5), ()):
                            act.wait_ge(k_copied, f + 1)
                            nc.scalar.activation(m.kexp[0:64, fu, :, 0, g, :], keys_of(fu)[0:64, :].rearrange("p (b k) -> p b k", b=UB), ACT.Identity,
                                                 bias=m.bkg[0:64, n_att, g:g + 1], scale=m.gmask[0:64, g:g + 1]).then_inc(k_ready, 1)
                    if cross and c == 6 and live(f - 3, UNITS):
                        wait(act, xn2_turned, f - 2)
                        wait(act, logits_ready, f - 3)
                        nc.scalar.activation(xn2t[:, :], bank(6)[:, :], ACT.Copy).then_inc(xn2_copied, 1)
                    if cross and c == 7 and live(f - 2, UNITS):
                        wait(act, c2_turned, f - 1)
                        wait(act, o_ready, f - 2)
                        for j in range(2):
                            for bp in range(2):
                                nc.scalar.activation(c2t[64 * j:64 * j + 64, :, bp, :],
                                                     bank(6)[64 * bp:64 * bp + 64, :].rearrange(
                                                         "p (b j q) -> p b j q", j=2, q=T)[:, :, j, :],
                                                     ACT.Copy).then_inc(c2_copied, 1)
                    if live(n - 2, B):
                        wait(act, turned, n - 1)
                        wait(act, out_ready, n - 3)
                        nc.scalar.activation(pts[:, c % 2, :, :], pt[c % 2][:, :, :], ACT.Copy).then_inc(turned_copied, 1)
                    if live(n, B):
                        wait(act, shifted, n + 1)
                        nc.scalar.activation(sh[:, c % 4, :], sh[:, c % 4, :], ACT.Exp).then_inc(probs_ready, 1)
            units(act, unit)

        @block.vector
        def _(dve):
            def x_tiles(f, fu):
                if cross:
                    return [x_of(m, f)[:, t, :] for t in range(UT)]
                return [xin[:, fu, t, :] for t in range(UT)]

            def stats_x(f, fu):
                src = x_tiles(f, fu)
                for t in range(UT):
                    nc.vector.bn_stats(stats[:, t, :], src[t]).then_inc(stats_ready, 1)

            def moments_x(f):
                for t in range(UT):
                    wait_apart(dve, stats_ready, UT * f + t + 1)
                    nc.vector.bn_aggr(moments[:, t, :], stats[:, t, :]).then_inc(moments_ready, 1)
                guess_rstd(nc, dve, moments[:, :, 1], veps[:, :], rstd[:, :], moments_ready, guessed, f)

            def norm_x(f, fu):
                dve.wait_ge(refined, 4 * NEWTON * (f + 1))
                wait(dve, xt_ready, f)
                src = x_tiles(f, fu)
                for t in range(UT):
                    nc.vector.tensor_scalar(xn[:, t, :], src[t], moments[:, t, 0:1], rstd[:, t:t + 1], ALU.subtract, ALU.mult)\
                        .then_inc(xn_ready, 1)

            def spread_q(f, fu, j, classes):
                dve.wait_ge(q_done, f + 1)
                for c in classes:
                    r = slice(32 * c, 32 * c + 32)
                    nc.vector.tensor_scalar(m.qexp[r, fu, :, c, :], bank(j)[r, :].rearrange("p (b q) -> p b q", b=UB),
                                            m.bqk[r, n_att, 0:1], HD ** -0.5, ALU.add, ALU.mult)\
                        .then_inc(*((q_ready, 1) if c == C - 1 else (q_part, 1)))

            q_part = sem("q_part")

            def spread_v(f, fu, j):
                dve.wait_ge(v_done, f + 1)
                for gh in range(2):
                    r = slice(64 * gh, 64 * gh + 64)
                    view = lambda t: t.rearrange("p (x c d) -> p x c d", c=C, d=HD)
                    out = m.vb[r, fu, :, :, gh, 0:HD].rearrange("p (x j) c d -> p x (j c) d", j=NPAIR)
                    nc.vector.tensor_tensor(out, view(bank(j)[r, :]), view(m.bv[r, n_att, :]), ALU.add).then_inc(v_ready, 1)

            def late(f, c):
                z = f - 3
                if not cross or not live(z, UNITS):
                    return
                if c == 0:
                    wait_apart(dve, o_added, z + 1)
                    for t in range(UT):
                        nc.vector.bn_stats(stats2[:, t, :], x_of(m, z)[:, t, :]).then_inc(stats2_ready, 1)
                    wait(dve, kept, 2 * z)
                    for t in range(UT):
                        wait_apart(dve, stats2_ready, UT * z + t + 1)
                        nc.vector.bn_aggr(moments2[:, t, :], stats2[:, t, :]).then_inc(moments2_ready, 1)
                    guess_rstd(nc, dve, moments2[:, :, 1], veps2[:, :], rstd2[:, :], moments2_ready, guessed2, z)
                if c == 2:
                    wait(dve, refined2, 4 * NEWTON * (z + 1))
                    wait(dve, xn2_turned, z)
                    for t in range(UT):
                        nc.vector.tensor_scalar(xn2[:, t, :], x_of(m, z)[:, t, :], moments2[:, t, 0:1], rstd2[:, t:t + 1],
                                                ALU.subtract, ALU.mult).then_inc(xn2_ready, 1)
                if c == 7:
                    wait_apart(dve, logits_ready, z + 1)
                    nc.vector.tensor_copy(m.lg[:, bass.ds(UT * z, UT), :], bank(7)[:, 0:UT * E].rearrange("p (t e) -> p t e", e=E))\
                        .then_inc(logits_read, 1)

            def front(f, fu, c):
                if not live(f, UNITS):
                    return
                if cross:
                    if c == 0:
                        dve.wait_ge(y_ready, f + 1)
                        dve.wait_ge(x_biased, f + 1)
                        nc.vector.tensor_tensor(x_of(m, f), bank(0)[:, :].rearrange("p (q n) -> p q n", q=UT), xin[:, fu, :, :], ALU.add).then_inc(x1_ready, 1)
                        wait_apart(dve, x1_ready, f + 1)
                        stats_x(f, fu)
                    if c == 1:
                        moments_x(f)
                    if c == 3:
                        norm_x(f, fu)
                    if c == 4:
                        spread_v(f, fu, 3)
                    if c == 5:
                        spread_q(f, fu, 5, range(C))
                else:
                    if known(f) and f == 0 and c == 0:
                        dve.wait_ge(x_loaded[0], 16)
                        stats_x(0, 0)
                        moments_x(0)
                    if c == 1:
                        norm_x(f, fu)
                    if c == 5:
                        spread_q(f, fu, 2, range(2))
                    if c == 6:
                        spread_q(f, fu, 2, range(2, C))
                    if c == 7:
                        spread_v(f, fu, 3)
                    if c == 3 and live(f + 1, UNITS):
                        dve.wait_ge(x_loaded[1 - fu], 16 * ((f + 1) // 2 + 1 if known(f) else pair[0] + 1 + fu))
                        stats_x(f + 1, 1 - fu)
                        moments_x(f + 1)

            def shift(n, c):
                if not live(n, B):
                    return
                dve.wait_ge(scores_ready, n + 1)
                src = sc[c % 2][:, :, :, :].rearrange("p j g k -> p (j g) k")
                nc.vector.tensor_reduce(mx[:, c % 2, :], src, AX.X, ALU.max).then_inc(max_ready, 1)
                dve.wait_ge(max_ready, n + 1)
                wait(dve, turned, n - 3)
                nc.vector.tensor_tensor(sh[:, c % 4, :].rearrange("p (h k) -> p h k", k=T), src,
                                        mx[:, c % 2, :].unsqueeze(2).broadcast_to([P, NPAIR * G, T]), ALU.subtract)\
                    .then_inc(shifted, 1)

            def normalize(n, c, su, u):
                if not live(n, B):
                    return
                pairs_done = 4 * su + (c + 1) // 2
                wait(dve, out_read, n - 1)
                dve.wait_ge(out_ready, n + 1)
                o = po_view(c // 2)
                nc.vector.reciprocal(rec[:, :, :, :], o[:, :, :, :, HD]).then_inc(recip_ready, 1)
                dve.wait_ge(recip_ready, pairs_done)
                for j in range(2):
                    r = slice(64 * j, 64 * j + 64)
                    if cross:
                        if c == 1:
                            wait(dve, c2_turned, su - 1)
                        out = c2[r, u, c - 1:c + 1, :, :]
                    else:
                        out = m.ctx[r, :, :, bass.ds(n - 1, 2)].rearrange("p h d b -> p b h d")
                    nc.vector.tensor_tensor(out, o[r, :, :, j, 0:HD], rec[r, :, :, j].unsqueeze(3).broadcast_to([64, 2, H // 2, HD]),
                                            ALU.mult).then_inc(out_read, 1)

            def add_out(f, fu, c):
                if cross and c == 7 and live(f - 2, UNITS):
                    wait(dve, o_ready, f - 1)
                    wait(dve, x1_biased, f - 1)
                    row = x_of(m, f - 2)
                    nc.vector.tensor_tensor(row, bank(7)[:, :].rearrange("p (q n) -> p q n", q=UT), row, ALU.add).then_inc(o_added, 1)

            pair = [None]

            def unit(su, u):
                f, fu = su + 1, 1 - u
                for c in range(UB):
                    n = UB * su + c
                    if c == 7:
                        late(f, c)
                    shift(n, c)
                    if (c - 4) % 2 == 1:
                        normalize(n - 4, (c - 4) % 8, su if c >= 4 else su - 1, u if c >= 4 else fu)
                    if c < 7:
                        late(f, c)
                    front(f, fu, c)
                    add_out(f, fu, c)

            if cross:
                lay_table(nc, m, m.maskf, laid)
            unit(-1, 1)
            unit(0, 0)
            unit(1, 1)
            with dve.Fori(1, UNITS // 2 - 1) as k:
                pair[0] = k
                unit(2 * k, 0)
                pair[0] = k + 1
                unit(2 * k + 1, 1)
            unit(UNITS - 2, 0)
            unit(UNITS - 1, 1)
            unit(UNITS, 0)
            unit(UNITS + 1, 1)


EXACT = "counts to 512, which float16 holds exactly"


def routing(nc, a, m):
    with ExitStack() as stack:
        s = Memory(nc)
        stack.enter_context(s.ctx)
        tables = s.sem("tables")
        exp_ready, counts_ready, counted, step = (s.sem(n) for n in ("exp_ready", "counts_ready", "counted", "step"))
        shifted_logits, probs_moved, thr_back, hot_ready, counted_hot = (
            s.sem(n) for n in ("shifted_logits", "probs_moved", "thr_back", "hot_ready", "counted_hot"))
        probs_done, thr_done, rows_done, slots_done, scattered = (
            s.sem(n) for n in ("probs_done", "thr_done", "rows_done", "slots_done", "scattered"))
        ps_c = s.ps("ps_c", [P, 2, E * UNITS])
        ps_n = s.ps("ps_n", [P, 512])
        ps_w = s.ps("ps_w", [P, E, TILES])
        ps_s = s.ps("ps_s", [P, E, TILES])
        lg = m.lg
        prx = s.sb("prx", [P, CAP // 2])
        hitx = s.sb("hitx", [P, CAP // 2])
        hitp, hita = (s.sb(n, [P, CAP // 2 - SHARE]) for n in ("hitp", "hita"))
        thrx = s.sb("thrx", [P, 1])
        candx, reached = (s.sb(n, [P, 3]) for n in ("candx", "reached"))
        cntx = s.sb("cntx", [P, 4], F16)
        sameh = s.sb("sameh", [P, P], F16)
        flagx = s.sb("flagx", [P, 3], I32)
        levels = s.sb("levels", [P, 3 * ROUNDS], I32)
        thr_rows = s.sb("thr_rows", [P, P])
        cands_ready, third_found, third_counted = (s.sem(n) for n in ("cands_ready", "third_found", "third_counted"))
        same = s.sb("same", [P, P])
        within = s.sb("within", [P, E, TILES])
        hot = s.sb("hot", [P, E, TILES])
        hotb = s.sb("hotb", [P, E, TILES], BF16)
        carry = s.sb("carry", [P, E, TILES])
        upto = s.sb("upto", [P, E, TILES])
        used = s.sb("used", [P, E])
        usedi = s.sb("usedi", [P, E], I32)
        ends = s.sb("ends", [P, E])
        starts = s.sb("starts", [P, E])
        ones8 = s.sb("ones8", [P, E])
        slots = s.sb("slots", [P, TILES], I32)
        tau = s.sb("tau", [P, NT])
        index = s.sb("index", [P, TILES], I32)
        past = s.sb("past", [P, NT, E])
        tile_e = s.sb("tile_e", [P, NT])
        pr = s.sb("pr", [P, E, TILES])
        red = s.sb("red", [P, TILES])
        thr = s.sb("thr", [P, E])
        hit = s.sb("hit", [P, TILES, E])
        cnt = s.sb("cnt", [P, E])
        above = s.sb("above", [P, E, TILES])
        tie = s.sb("tie", [P, E, TILES])
        tierow = s.sb("tierow", [P, E, UNITS], BF16)
        rank = s.sb("rank", [P, E, TILES])
        base = s.sb("base", [P, E, UNITS])
        carryu = s.sb("carryu", [P, E, UNITS])
        want = s.sb("want", [P, E])
        maski = s.sb("r_maski", [P, E, TILES], I32)
        key = s.sb("key", [P, E, TILES])
        best = s.sb("best", [P, TILES])
        free = s.sb("free", [P, TILES], I32)
        taken = s.sb("taken", [P, TILES, E])
        carryt = s.sb("carryt", [P, TILES, E])
        block = stack.enter_context(nc.Block())

        @block.sync
        def _(sp):
            sp.dma_start(same[:, :], a["same_expert"]).then_inc(tables, 16)
            sp.dma_start(tau[:, :], a["tile_numbers"].partition_broadcast(P)).then_inc(tables, 16)
            sp.dma_start(index[:, :], a["token_index"]).then_inc(tables, 16)
            sp.dma_start(levels[:, :], a["threshold_levels"].partition_broadcast(P)).then_inc(tables, 16)
            sp.wait_ge(probs_done, 1)
            for e in range(E):
                sp.dma_start(prx[16 * e:16 * e + 16, :], pr[:, e, :]).then_inc(probs_moved, 16)
            sp.wait_ge(tables, 16 * 4)

        @block.gpsimd
        def _(pool):
            pool.wait_ge(probs_moved, 16 * E)
            for i in range(ROUNDS):
                pool.wait_ge(cands_ready, i + 1)
                nc.gpsimd.tensor_scalar(hitp[:, :], prx[:, SHARE:], candx[:, 2:3], None, ALU.is_ge).then_inc(third_found, 1)
            pool.wait_ge(slots_done, 1)
            pool.wait_ge(rows_done, 2)
            pool.wait_ge(m.filled, 16)

            for t in range(TILES):
                nc.gpsimd.indirect_dma_start(m.sorted, bass.IndirectOffsetOnAxis(ap=slots[:, t:t + 1], axis=0),
                                             m.rows[:, t // UT, t % UT, :], None).then_inc(scattered, 16)
            pool.wait_ge(scattered, 16 * TILES)

        @block.tensor
        def _(pe):
            pe.wait_ge(tables, 16 * 4)
            def count(i):
                pe.wait_ge(counts_ready, i + 1)
                pe.wait_ge(third_counted, i + 1)
                nc.tensor.matmul(ps_c[:, 0, 0:3], sameh[:, :], cntx[:, 0:3], start=True, stop=False)
                nc.tensor.matmul(ps_c[:, 0, 2:3], sameh[:, :], cntx[:, 3:4], start=False, stop=True).then_inc(counted, 1)
            for i in range(ROUNDS):
                count(i)
            pe.wait_ge(thr_done, 1)
            nc.tensor.transpose(ps_n[:, 0:P], thr_rows[:, :], m.ident[:, :]).then_inc(thr_back, 1)
            pe.wait_ge(counts_ready, ROUNDS + 1)
            nc.tensor.matmul(ps_c[:, 0, 0:E], m.ones[:, :], cnt[:, :], start=True, stop=True).then_inc(counted, 1)
            pe.wait_ge(counts_ready, ROUNDS + 2)
            rows = tierow[:, :, :].rearrange("p e h -> p (e h)")
            nc.tensor.matmul(ps_c[:, 0, :], m.beforeb[:, :], rows, start=True, stop=True)
            nc.tensor.matmul(ps_c[:, 1, :], m.onesb[:, :], rows, start=True, stop=True).then_inc(counted, 1)
            pe.wait_ge(hot_ready, 1)
            nc.tensor.matmul(ps_w[:, :, :], m.beforeb[:, :], hotb[:, :, :], start=True, stop=True).then_inc(counted_hot, 1)
            nc.tensor.matmul(ps_s[:, :, :], m.onesb[:, :], hotb[:, :, :], start=True, stop=True).then_inc(counted_hot, 1)

        @block.scalar
        def _(act):
            act.wait_ge(shifted_logits, 1)
            nc.scalar.activation(lg[:, :, :], lg[:, :, :], ACT.Exp).then_inc(exp_ready, 1)
            for i in range(ROUNDS):
                act.wait_ge(third_found, i + 1)
                if i:
                    act.wait_ge(third_counted, i)
                with nc.allow_low_precision(reason=EXACT):
                    nc.scalar.activation(hita[:, :], hitp[:, :], ACT.Copy, accum_out=cntx[:, 3:4]).then_inc(third_counted, 1)

        @block.vector
        def _(dve):
            done = [0]

            def then(ins):
                done[0] += 1
                ins.then_inc(step, 1)
                dve.wait_ge(step, done[0])

            wide = lambda t: t.unsqueeze(2).broadcast_to([P, TILES, E])
            per_expert = lambda t: t[:, :].unsqueeze(2).broadcast_to([P, E, TILES])
            per_token = lambda t: t[:, :].unsqueeze(1).broadcast_to([P, E, TILES])
            then(nc.vector.tensor_reduce(red[:, :], lg[:, :, :], AX.X, ALU.max))
            nc.vector.tensor_tensor(lg[:, :, :], lg[:, :, :], wide(red[:, :]), ALU.subtract).then_inc(shifted_logits, 1)
            dve.wait_ge(exp_ready, 1)
            then(nc.vector.tensor_reduce(red[:, :], lg[:, :, :], AX.X, ALU.add))
            then(nc.vector.reciprocal(red[:, :], red[:, :]))
            nc.vector.tensor_tensor(pr[:, :, :].rearrange("p e t -> p t e"), lg[:, :, :], wide(red[:, :]), ALU.mult).then_inc(probs_done, 1)
            then(nc.vector.memset(thrx[:, :], 0.0))
            for ones_but_first in (carry, carryu, carryt):
                then(nc.vector.memset(ones_but_first[:, :, :], 1.0))
                then(nc.vector.memset(ones_but_first[:, :, 0:1], 0.0))
            then(nc.vector.memset(ones8[:, :], 1.0))
            then(nc.vector.memset(key[:, :, :], -1.0))
            dve.wait_ge(tables, 16 * 4)
            then(nc.vector.tensor_copy(sameh[:, :], same[:, :]))
            nc.vector.tensor_copy(m.rows[:, :, :, INDEX].rearrange("p u q -> p (u q)").bitcast(I32), index[:, :]).then_inc(rows_done, 1)
            dve.wait_ge(probs_moved, 16 * E)
            for i in range(ROUNDS):
                nc.vector.tensor_tensor(candx[:, :].bitcast(I32), levels[:, 3 * i:3 * i + 3], thrx[:, :].bitcast(I32).broadcast_to([P, 3]),
                                        ALU.bitwise_or).then_inc(cands_ready, 1)
                dve.wait_ge(cands_ready, i + 1)
                with nc.allow_low_precision(reason=EXACT):
                    then(nc.vector.tensor_scalar(hitx[:, :], prx[:, :], candx[:, 0:1], None, ALU.is_ge, ALU.add, accum_out=cntx[:, 0:1]))
                with nc.allow_low_precision(reason=EXACT):
                    then(nc.vector.tensor_scalar(hitx[:, :], prx[:, :], candx[:, 1:2], None, ALU.is_ge, ALU.add, accum_out=cntx[:, 1:2]))
                with nc.allow_low_precision(reason=EXACT):
                    nc.vector.tensor_scalar(hitx[:, 0:SHARE], prx[:, 0:SHARE], candx[:, 2:3], None, ALU.is_ge, ALU.add, accum_out=cntx[:, 2:3])\
                        .then_inc(counts_ready, 1)
                then(nc.vector.tensor_copy(reached[:, :], thrx[:, :].broadcast_to([P, 3])))
                dve.wait_ge(counted, i + 1)
                then(nc.vector.tensor_scalar(flagx[:, :], ps_c[:, 0, 0:3], float(CAP), None, ALU.is_ge))
                then(nc.vector.copy_predicated(reached[:, :], flagx[:, :], candx[:, :]))
                then(nc.vector.tensor_reduce(thrx[:, :], reached[:, :], AX.X, ALU.max))
            nc.vector.tensor_copy(thr_rows[:, :], thrx[:, :].broadcast_to([P, P])).then_inc(thr_done, 1)
            dve.wait_ge(thr_back, 1)
            then(nc.vector.tensor_copy(thr[:, :], ps_n[:, 0:P:P // E]))
            then(nc.vector.tensor_tensor(above[:, :, :], pr[:, :, :], per_expert(thr), ALU.is_gt))
            nc.vector.tensor_reduce(cnt[:, :], above[:, :, :], AX.X, ALU.add).then_inc(counts_ready, 1)
            dve.wait_ge(counted, ROUNDS + 1)
            then(nc.vector.tensor_scalar(want[:, :], ps_c[:, 0, 0:E], -1.0, float(CAP), ALU.mult, ALU.add))
            then(nc.vector.tensor_tensor(tie[:, :, :], pr[:, :, :], per_expert(thr), ALU.is_equal))
            by_parity = lambda t: t[:, :, :].rearrange("p e (h j) -> p e j h", j=2)
            of_tile = lambda t, q: t[:, :, :].rearrange("p e (j h q) -> p e j h q", j=2, q=UT)[:, :, :, :, q]
            by_unit = lambda t: t[:, :, :].rearrange("p e (h q) -> p e h q", q=UT)
            then(nc.vector.tensor_reduce(base[:, :, :], by_unit(tie), AX.X, ALU.add))
            nc.vector.tensor_copy(by_parity(tierow), base[:, :, :].rearrange("p e (j h) -> p e j h", j=2)).then_inc(counts_ready, 1)
            dve.wait_ge(counted, ROUNDS + 2)
            in_unit = ps_c[:, 0, :].rearrange("p (e h) -> p e h", e=E)
            of_unit = ps_c[:, 1, :].rearrange("p (e h) -> p e h", e=E)
            then(nc.vector.tensor_tensor_scan(base[:, :, :].rearrange("p e h -> p (e h)"), carryu[:, :, :].rearrange("p e h -> p (e h)"),
                                              ps_c[:, 1, :], 0.0, ALU.mult, ALU.add))
            then(nc.vector.tensor_tensor(base[:, :, :], base[:, :, :], of_unit, ALU.subtract))
            then(nc.vector.tensor_tensor(base[:, :, :], in_unit, base[:, :, :], ALU.add))
            then(nc.vector.tensor_tensor(of_tile(rank, 0), by_parity(base), of_tile(tie, 0), ALU.add))
            for q in range(1, UT):
                then(nc.vector.tensor_tensor(by_unit(rank)[:, :, :, q], by_unit(rank)[:, :, :, q - 1], by_unit(tie)[:, :, :, q], ALU.add))
            then(nc.vector.tensor_tensor(rank[:, :, :], rank[:, :, :], per_expert(want), ALU.is_le))
            then(nc.vector.tensor_tensor(tie[:, :, :], tie[:, :, :], rank[:, :, :], ALU.mult))
            then(nc.vector.tensor_tensor(maski[:, :, :], above[:, :, :], tie[:, :, :], ALU.add))
            then(nc.vector.copy_predicated(key[:, :, :], maski[:, :, :], pr[:, :, :]))
            then(nc.vector.tensor_reduce(best[:, :], key[:, :, :].rearrange("p e t -> p t e"), AX.X, ALU.max))
            then(nc.vector.tensor_scalar(free[:, :], best[:, :], 0.0, None, ALU.is_lt))
            then(nc.vector.copy_predicated(key[:, :, :], per_token(free), pr[:, :, :]))
            then(nc.vector.tensor_reduce(best[:, :], key[:, :, :].rearrange("p e t -> p t e"), AX.X, ALU.max))
            then(nc.vector.tensor_tensor(hit[:, :, :], key[:, :, :].rearrange("p e t -> p t e"), wide(best[:, :]), ALU.is_equal))
            then(nc.vector.tensor_tensor_scan(taken[:, :, :].rearrange("p t e -> p (t e)"), carryt[:, :, :].rearrange("p t e -> p (t e)"),
                                              hit[:, :, :].rearrange("p t e -> p (t e)"), 0.0, ALU.mult, ALU.add))
            then(nc.vector.scalar_tensor_tensor(out=hot[:, :, :].rearrange("p e t -> p t e"), in0=taken[:, :, :], scalar=1.0,
                                                in1=hit[:, :, :], op0=ALU.is_equal, op1=ALU.mult))
            nc.vector.tensor_copy(hotb[:, :, :], hot[:, :, :]).then_inc(hot_ready, 1)
            nc.vector.tensor_copy(m.rows[:, :, :, WEIGHT].rearrange("p u q -> p (u q)"), best[:, :]).then_inc(rows_done, 1)
            dve.wait_ge(counted_hot, 2)
            flat = lambda t: t[:, :, :].rearrange("p e t -> p (e t)")
            then(nc.vector.tensor_tensor_scan(flat(upto), flat(carry), flat(ps_s), 0.0, ALU.mult, ALU.add))
            then(nc.vector.tensor_tensor(within[:, :, :], upto[:, :, :], ps_s[:, :, :], ALU.subtract))
            then(nc.vector.tensor_tensor(within[:, :, :], within[:, :, :], ps_w[:, :, :], ALU.add))
            then(nc.vector.tensor_scalar(usedi[:, :], upto[:, :, TILES - 1], float(P - 1), None, ALU.add))
            then(nc.vector.tensor_scalar(usedi[:, :], usedi[:, :], 7, None, ALU.arith_shift_right))
            then(nc.vector.tensor_copy(used[:, :], usedi[:, :]))
            then(nc.vector.tensor_tensor_scan(ends[:, :], ones8[:, :], used[:, :], 0.0, ALU.mult, ALU.add))
            then(nc.vector.tensor_tensor(starts[:, :], ends[:, :], used[:, :], ALU.subtract))
            then(nc.vector.tensor_scalar(starts[:, :], starts[:, :], float(P), None, ALU.mult))
            then(nc.vector.tensor_tensor(within[:, :, :], within[:, :, :], per_expert(starts), ALU.add))
            then(nc.vector.tensor_tensor(within[:, :, :], within[:, :, :], hot[:, :, :], ALU.mult))
            then(nc.vector.tensor_reduce(red[:, :], within[:, :, :].rearrange("p e t -> p t e"), AX.X, ALU.add))
            nc.vector.tensor_copy(slots[:, :], red[:, :]).then_inc(slots_done, 1)
            then(nc.vector.tensor_tensor(past[:, :, :], tau[:, :].unsqueeze(2).broadcast_to([P, NT, E]),
                                         ends[:, :].unsqueeze(1).broadcast_to([P, NT, E]), ALU.is_ge))
            then(nc.vector.tensor_reduce(tile_e[:, :], past[:, :, :], AX.X, ALU.add))
            then(nc.vector.tensor_scalar(m.tile_weights[:, :], tile_e[:, :], float(E - 1), float(FF), ALU.min, ALU.mult))


def experts(nc, a, m, out):
    with ExitStack() as stack:
        s = Memory(nc)
        stack.enter_context(s.ctx)
        w_loaded, xn_ready, xt_ready, xt_copied = (s.sem("e_" + n) for n in ("w_loaded", "xn_ready", "xt_ready", "xt_copied"))
        h_ready, gelu_ready, turned, ht_copied = (s.sem("e_" + n) for n in ("h_ready", "gelu_ready", "turned", "ht_copied"))
        y_ready, o_ready = s.sem("e_y_ready"), s.sem("e_o_ready")
        row_loaded = [s.sem(f"row_loaded{i}") for i in range(RING)]
        scattered = [s.sem(f"out_scattered{i}") for i in range(RING)]
        px = [s.ps(f"px{i}", [P, P]) for i in range(2)]
        ph = [s.ps(f"ph{i}", [P, FF]) for i in range(2)]
        pg = [s.ps(f"pg{i}", [P, 2, P]) for i in range(2)]
        py = [s.ps(f"py{i}", [P, D]) for i in range(2)]
        w1 = s.sb("w1", [P, E, FF])
        w2 = s.sb("w2", [P, E, 2, D])
        row = s.sb("row", [P, RING, ROW])
        xn = s.sb("e_xn", [P, 2, D])
        xt = s.sb("e_xt", [P, 2, P])
        hs = s.sb("hs", [P, 2, FF])
        ht = s.sb("ht", [P, 2, 2, P])
        orow = s.sb("orow", [P, RING, D])
        block = stack.enter_context(nc.Block())

        def steps(eng, step, lag):
            for c in range(RING):
                step(c, c, 0)
            with eng.Fori(1, NT // RING) as k:
                for c in range(RING):
                    step(RING * k + c, c, k)
            for c in range(lag):
                step(NT + c, c, NT // RING)

        @block.sync
        def _(sp):
            sp.dma_start(w1[:, :, :], a["w1"]).then_inc(w_loaded, 16)
            sp.dma_start(w2[:, :, :, :], a["w2"]).then_inc(w_loaded, 16)

            def load(n, c, k):
                wait(sp, scattered[c], 16 * k)
                sp.dma_start(row[:, c, :], m.sorted[bass.ds(P * n, P), :]).then_inc(row_loaded[c], 16)
            steps(sp, load, 0)

        @block.tensor
        def _(pe):
            pe.wait_ge(w_loaded, 32)

            weights = {}
            w1_flat = w1[:, :, :].rearrange("p e n -> p (e n)")
            w2_flat = w2[:, :, :, :].rearrange("p e f n -> p (e f n)")

            def weights_of(i):
                return pe.value_load(m.tile_weights[0:1, bass.ds(i, 1)], min_val=0, max_val=(E - 1) * FF)

            def step(n, c, k):
                if live(n, NT):
                    wait(pe, xn_ready, n + 1)
                    nc.tensor.transpose(px[c % 2][:, :], xn[:, c % 2, :], m.ident[:, :]).then_inc(xt_ready, 1)
                i = n - 4
                if live(i, NT):
                    if c < 4:
                        weights[c - 4] = weights_of(i)
                    wait(pe, ht_copied, i + 1)
                    for f in range(2):
                        last = nc.tensor.matmul(py[c % 2][:, :], ht[:, c % 2, f, :],
                                                w2_flat[:, D * f:][:, bass.ds(weights[c - 4], D)], start=(f == 0), stop=(f == 1))
                    last.then_inc(y_ready, 1)
                i = n - 1
                if live(i, NT):
                    if c == 0:
                        weights[-1] = weights_of(i)
                    wait(pe, xt_copied, i + 1)
                    nc.tensor.matmul(ph[(c - 1) % 2][:, :], xt[:, (c - 1) % 2, :], w1_flat[:, bass.ds(weights[c - 1], FF)],
                                     start=True, stop=True).then_inc(h_ready, 1)
                i = n - 2
                if live(i, NT):
                    wait(pe, gelu_ready, i + 1)
                    for f in range(2):
                        last = nc.tensor.transpose(pg[c % 2][:, f, :], hs[:, c % 2, P * f:P * f + P], m.ident[:, :])
                    last.then_inc(turned, 1)
                if live(n, NT) and c < RING - 1:
                    weights[c] = weights_of(n)
            steps(pe, step, 4)

        @block.scalar
        def _(act):
            def step(n, c, k):
                if live(n, NT):
                    wait(act, xt_ready, n + 1)
                    wait(act, h_ready, n - 1)
                    nc.scalar.activation(xt[:, c % 2, :], px[c % 2][:, :], ACT.Copy).then_inc(xt_copied, 1)
                i = n - 1
                if live(i, NT):
                    wait(act, h_ready, i + 1)
                    wait(act, turned, i - 1)
                    nc.scalar.activation(hs[:, (c - 1) % 2, :], ph[(c - 1) % 2][:, :], ACT.Gelu).then_inc(gelu_ready, 1)
            steps(act, step, 1)

        @block.vector
        def _(dve):
            def step(n, c, k):
                if live(n, NT):
                    dve.wait_ge(row_loaded[c], 16 * (k + 1))
                    wait(dve, xt_copied, n - 1)
                    nc.vector.tensor_scalar(xn[:, c % 2, :], row[:, c, 0:D], row[:, c, MEAN:MEAN + 1], row[:, c, RSTD:RSTD + 1],
                                            ALU.subtract, ALU.mult).then_inc(xn_ready, 1)
                i, at = n - 5, (c - 5) % RING
                if live(i, NT):
                    wait(dve, y_ready, i + 1)
                    wait(dve, scattered[at], 16 * (k if c >= 5 else k - 1))
                    nc.vector.scalar_tensor_tensor(out=orow[:, at, :], in0=py[(c - 5) % 2][:, :], scalar=row[:, at, WEIGHT:WEIGHT + 1],
                                                   in1=row[:, at, 0:D], op0=ALU.mult, op1=ALU.add).then_inc(o_ready, 1)
                i = n - 3
                if live(i, NT):
                    wait(dve, turned, i + 1)
                    wait(dve, y_ready, i - 1)
                    nc.vector.tensor_copy(ht[:, (c - 3) % 2, :, :], pg[(c - 3) % 2][:, :, :]).then_inc(ht_copied, 1)
            steps(dve, step, 5)

        @block.gpsimd
        def _(pool):
            def scatter(n, c, k):
                wait_apart(pool, o_ready, n + 1)
                nc.gpsimd.indirect_dma_start(out, bass.IndirectOffsetOnAxis(ap=row[:, c, INDEX:ROW].bitcast(I32), axis=0),
                                             orow[:, c, :], None, bounds_check=B * T - 1, oob_is_err=False).then_inc(scattered[c], 16)
            steps(pool, scatter, 0)
            for c in range(RING):
                pool.wait_ge(scattered[c], 16 * (NT // RING))


def decoder_layer(nc, a, out):
    m = Memory(nc)
    sorted_rows = nc.dram_tensor("sorted_rows", (NT * P, ROW), F32, kind="Internal").ap()
    with m.ctx:
        m.filled = m.sem("filled")
        m.consts = m.sb("consts", [P, 3, P])
        m.ident, m.dup, m.before = (m.consts[:, i, :] for i in range(3))
        m.gmask = m.sb("gmask", [P, G])
        m.bkg = m.sb("bkg", [P, 2, G])
        m.beforeb = m.sb("beforeb", [P, P], BF16)
        m.ones = m.sb("ones", [P, P])
        m.onesb = m.sb("onesb", [P, P], BF16)
        m.wg = m.sb("wg", [P, E])
        m.tb = m.sb("tb", [P, T])
        m.gates = m.sb("gates", [P, 4])
        m.maski = m.sb("maski", [P, T], I32)
        m.maskf = m.sb("maskf", [P, T])
        m.bo_row = m.sb("bo_row", [P, 2, D])
        m.wo = m.sb("wo", [P, 2, D])
        m.wqkv = m.sb("wqkv", [P, 2, 3, D])
        m.bqk = m.sb("bqk", [P, 2, 2])
        m.bv = m.sb("bv", [P, 2, UB * T])
        m.rows = m.sb("rows", [P, UNITS, UT, ROW])
        m.x = m.rows[:, :, :, 0:D]
        m.lg = m.sb("lg", [P, TILES, E])
        m.pad = m.sb("pad", [P, ROW])
        m.tile_weights = m.sb("tile_weights", [P, NT], I32)
        m.sorted = sorted_rows
        m.ctx_ = m.sb("ctx", [P, H // 2, HD, B])
        att = ExitStack()
        keep, m.ctx = m.ctx, att
        m.ctxt = m.sb("ctxt", [P, H, UT, B])
        m.qexp = m.sb("qexp", [P, 2, UB, C, T])
        m.kexp = m.sb("kexp", [P, 2, UB, NPAIR, G, T])
        m.vb = m.sb("vb", [P, 2, UB * 4, 2, 2, OW])
        m.ctx = m.ctx_
        setup(nc, a, m)
        attention(nc, a, m, False)
        attention(nc, a, m, True)
        att.close()
        routing(nc, a, m)
        experts(nc, a, m, out)
        m.ctx = keep


def kernel(**inputs):
    import numpy as np
    import concourse.bacc as bacc
    from concourse.bass_utils import run_bass_kernel_spmd

    w = {k: np.asarray(v) for k, v in inputs.items()}
    at, xa = "L0_attn_", "L0_xattn_"
    pos = np.arange(T)
    rows = np.stack([w[at + "time_bias"][0, 0, 250 - q:250 - q + T] for q in range(T)])
    mask = w["mask_1x1xSxS2_ik0"][0, 0]
    dup = (pos[:, None] == pos[None, :]).astype(np.float32)
    heads = np.concatenate([np.arange(0, H, 2), np.arange(1, H, 2)])
    token_index = (P * UT * heads[None, :, None] + UT * np.arange(P)[:, None, None] + np.arange(UT)[None, None, :])
    token_index = token_index.reshape(P, TILES).astype(np.int32)
    arrays = {
        "x_tiles": w["x"].reshape(UNITS, UT, P, D),
        "x_rows": w["x"].reshape(UNITS, P, UT * D)[heads],
        "ctx_tiles": w["ctx_1024"].reshape(UNITS, UT, P, D)[heads],
        "consts": np.stack([np.eye(P, dtype=np.float32), np.tile(dup, (2, 2)),
                            (np.arange(P)[:, None] < np.arange(P)[None, :]).astype(np.float32)], axis=1),
        "group_mask": ((np.arange(P)[:, None] % 32) // HD == np.arange(G)[None, :]).astype(np.float32),
        "wg": w["L0_ffn_Wg"],
        "same_expert": (np.arange(P)[:, None] // 16 == np.arange(P)[None, :] // 16).astype(np.float32),
        "tile_numbers": np.arange(NT, dtype=np.float32),
        "token_index": token_index,
        "threshold_levels": np.array([v << (BITS - 2 - 2 * i) for i in range(ROUNDS) for v in (1, 2, 3)], np.int32),
        "time_tile": np.concatenate([rows, rows]),
        "gates": np.concatenate([w[at + "et_gate"].reshape(1), w[at + "is_gate"].reshape(1)]),
        "mask_tile": np.concatenate([mask, mask]),
        "bo": np.stack([w[at + "bo"], w[xa + "bo"]]),
        "wo": np.stack([w[at + "Wo"].T, w[xa + "wo"].T.reshape(H // 2, 2, HD, D).transpose(1, 0, 2, 3).reshape(P, D)], axis=1),
        "w1": w["L0_ffn_W1"].transpose(1, 0, 2),
        "w2": w["L0_ffn_W2"].reshape(E, 2, P, D).transpose(2, 0, 1, 3),
    }
    by_class = np.arange(D).reshape(G, C, HD).transpose(1, 0, 2).reshape(D)
    weights, biases, value_biases = [], [], []
    for p, up in ((at, "W"), (xa, "w")):
        weights += [w[p + up + "q"].T[:, by_class], w[p + up + "k"].T[:, by_class], w[p + up + "v"].T]
        biases += [w[p + "bq"][by_class], w[p + "bk"][by_class]]
        value_biases.append(np.tile(w[p + "bv"].reshape(G // 2, 2, C * HD).transpose(1, 0, 2).reshape(2, -1), (1, UB)))
    arrays["wqkv"] = np.stack(weights, axis=1).reshape(P, 2, 3, D)
    arrays["bqk"] = np.stack(biases, axis=1).reshape(P, 2, 2)
    arrays["bv"] = np.stack(value_biases, axis=1)
    arrays = {k: np.ascontiguousarray(v) for k, v in arrays.items()}
    nc = bacc.Bacc("TRN2", target_bir_lowering=False, num_devices=1)
    aps = {k: nc.dram_tensor(k + "_dram", v.shape, mybir.dt.from_np(v.dtype), kind="ExternalInput").ap() for k, v in arrays.items()}
    out = nc.dram_tensor("out_dram", (B * T, D), F32, kind="ExternalOutput").ap()
    decoder_layer(nc, aps, out)
    r = run_bass_kernel_spmd(nc, [{k + "_dram": v for k, v in arrays.items()}], core_ids=[0])
    return r.results[0]["out_dram"].reshape(B, T, D)
```
